# Optimizing a Trainium2 kernel written in Bass

```python
import numpy as np
import jax
import jax.numpy as jnp

def _softmax(x, axis=-1):
    return jax.nn.softmax(x, axis=axis)

def _gelu(x):
    return jax.nn.gelu(x, approximate=True)

def _silu(x):
    return jax.nn.silu(x)

def _sigmoid(x):
    return jax.nn.sigmoid(x)

def _layernorm(x, axis=-1, eps=1e-05):
    m = jnp.mean(x, axis=axis, keepdims=True)
    v = jnp.var(x, axis=axis, keepdims=True)
    return (x - m) / jnp.sqrt(v + eps)

def _scatter_add(tgt, idx, src, axis=0):
    return tgt.at[idx].add(src)

def _segment_sum(src, seg, n):
    return jax.ops.segment_sum(src, seg, n)
kernel_name = 'mk_cond_resid_d4_seqx_r8_d177d1'

def setup_inputs(seed: int=0):
    np.random.seed(seed)
    _w = jnp.asarray

    def _rec_inputs():
        import jax
        import jax.numpy as jnp
        _rk = jax.random.key(seed)
        x = -0.000125 + 0.9999 * jax.random.normal(jax.random.fold_in(_rk, 1), (64, 32, 512), jnp.float32)
        _lenS = 32 - jax.random.randint(jax.random.fold_in(_rk, 7), (64,), 0, max(1, 32 // 4) + 1, jnp.int32)
        _lenS2 = 32 - jax.random.randint(jax.random.fold_in(_rk, 8), (64,), 0, max(1, 32 // 4) + 1, jnp.int32)
        itok_B_3_7 = jax.random.randint(jax.random.fold_in(_rk, 11), (64,), 3, 8, jnp.int32)
        itok_B_1_7 = jax.random.randint(jax.random.fold_in(_rk, 12), (64,), 1, 8, jnp.int32)
        itok_B_0_23 = jax.random.randint(jax.random.fold_in(_rk, 13), (64,), 0, 24, jnp.int32)
        itok_Bx16_0_63 = jax.random.randint(jax.random.fold_in(_rk, 14), (64, 16), 0, 64, jnp.int32)
        itok_B_207_1644 = jax.random.randint(jax.random.fold_in(_rk, 15), (64,), 207, 1645, jnp.int32)
        return (x, itok_B_3_7, itok_B_1_7, itok_B_0_23, itok_Bx16_0_63, itok_B_207_1644)
    x, itok_B_3_7, itok_B_1_7, itok_B_0_23, itok_Bx16_0_63, itok_B_207_1644 = _rec_inputs()

    def _L0_cond_setup():
        import jax, jax.numpy as jnp
        import numpy as np
        MAX_LORAS, OUT, IN = (8, 512, 512)
        B, S = (4, 256)
        key = jax.random.key(seed)
        k1, k2, k3 = jax.random.split(key, 3)
        x = jax.random.normal(k1, (B, S, IN), dtype=jnp.float32)
        weight = jax.random.normal(k2, (MAX_LORAS, OUT, IN), dtype=jnp.float32) * 0.02
        adapter_ids = jax.random.randint(k3, (B,), 0, MAX_LORAS, dtype=jnp.int32)
        return {'x': x, 'weight': weight, 'adapter_ids': adapter_ids}
    _L0_cond_all = _L0_cond_setup()
    _L0_cond_in = {k: v for k, v in _L0_cond_all.items() if k in ('weight',)}
    del _L0_cond_all

    def _L1_cond_setup():
        import jax, jax.numpy as jnp
        import numpy as np
        B, S, D_IN, D_OUT = (4, 256, 512, 512)
        N_ADAPTERS, MAX_RANK = (8, 16)
        key = jax.random.key(seed)
        ks = jax.random.split(key, 7)
        x = jax.random.normal(ks[0], (B, S, D_IN), dtype=jnp.float32)
        weight = jax.random.normal(ks[1], (D_OUT, D_IN), dtype=jnp.float32) * (1.0 / np.sqrt(D_IN))
        bias = jax.random.normal(ks[2], (D_OUT,), dtype=jnp.float32) * 0.01
        lora_a_weights = jax.random.normal(ks[3], (N_ADAPTERS, MAX_RANK, D_IN), dtype=jnp.float32) * (1.0 / np.sqrt(D_IN))
        lora_b_weights = jax.random.normal(ks[4], (N_ADAPTERS, D_OUT, MAX_RANK), dtype=jnp.float32) * 0.02
        scaling_factors = jax.random.uniform(ks[5], (N_ADAPTERS,), dtype=jnp.float32, minval=0.5, maxval=2.0)
        adapter_id = jax.random.randint(ks[6], (B,), 0, N_ADAPTERS, dtype=jnp.int64)
        return {'x': x, 'weight': weight, 'bias': bias, 'lora_a_weights': lora_a_weights, 'lora_b_weights': lora_b_weights, 'scaling_factors': scaling_factors, 'adapter_id': adapter_id}
    _L1_cond_all = _L1_cond_setup()
    _L1_cond_in = {k: v for k, v in _L1_cond_all.items() if k in ('weight', 'bias', 'lora_a_weights', 'lora_b_weights', 'scaling_factors')}
    del _L1_cond_all

    def _L2_cond_setup():
        import jax, jax.numpy as jnp
        import numpy as np
        R = 16
        ALPHA = 32
        SCALING = ALPHA / R
        SLOTS = 32
        IN_F = 512
        OUT_F = 512
        B, T = (8, 128)
        key = jax.random.key(seed)
        k1, k2, k3, k4, k5, k6 = jax.random.split(key, 6)
        x = jax.random.normal(k1, (B, T, IN_F), dtype=jnp.float32)
        adapter_mapping = jax.random.randint(k2, (B,), 0, SLOTS, dtype=jnp.int32)
        W = jax.random.normal(k3, (OUT_F, IN_F), dtype=jnp.float32) * 0.02
        b = jax.random.normal(k4, (OUT_F,), dtype=jnp.float32) * 0.02
        lora_As = jax.random.normal(k5, (SLOTS, IN_F, R), dtype=jnp.float32) * 0.02
        lora_Bs = jax.random.normal(k6, (SLOTS, R, OUT_F), dtype=jnp.float32) * 0.02
        return {'x': x, 'adapter_mapping': adapter_mapping, 'W': W, 'b': b, 'lora_As': lora_As, 'lora_Bs': lora_Bs}
    _L2_cond_all = _L2_cond_setup()
    _L2_cond_in = {k: v for k, v in _L2_cond_all.items() if k in ('W', 'b', 'lora_As', 'lora_Bs')}
    del _L2_cond_all

    def _L3_cond_setup():
        import jax, jax.numpy as jnp
        import numpy as np
        B, S, HID = (4, 128, 512)
        D, HQ, HK = (128, 32, 8)
        PAGES, PSIZE, NPP = (64, 32, 16)
        THETA = 10000.0
        EPS = 1e-06
        SCALE = 1.0 / float(np.sqrt(D))

        def _rmsnorm(t, w):
            var = jnp.mean(t * t, axis=-1, keepdims=True)
            return t * jax.lax.rsqrt(var + EPS) * w

        def _rope(t, pos):
            inv_freq = 1.0 / THETA ** (jnp.arange(0, D, 2, dtype=jnp.float32) / D)
            freqs = pos[..., None].astype(jnp.float32) * inv_freq
            cos = jnp.cos(freqs)[:, :, None, :]
            sin = jnp.sin(freqs)[:, :, None, :]
            t1, t2 = (t[..., :D // 2], t[..., D // 2:])
            return jnp.concatenate([t1 * cos - t2 * sin, t2 * cos + t1 * sin], axis=-1)
        key = jax.random.key(seed)
        ks = jax.random.split(key, 10)
        x = jax.random.normal(ks[0], (B, S, HID), jnp.float32)
        Wq = jax.random.normal(ks[1], (HQ * D, HID), jnp.float32) * 0.02
        Wk = jax.random.normal(ks[2], (HK * D, HID), jnp.float32) * 0.02
        Wv = jax.random.normal(ks[3], (HK * D, HID), jnp.float32) * 0.02
        Wo = jax.random.normal(ks[4], (HID, HQ * D), jnp.float32) * 0.02
        q_norm_w = jax.random.uniform(ks[5], (D,), jnp.float32)
        k_norm_w = jax.random.uniform(ks[6], (D,), jnp.float32)
        k_cache = jax.random.normal(ks[7], (PAGES, PSIZE, HK, D), jnp.float32)
        v_cache = jax.random.normal(ks[8], (PAGES, PSIZE, HK, D), jnp.float32)
        block_table = jnp.arange(B * NPP, dtype=jnp.int32).reshape(B, NPP)
        cache_seqlens = jax.random.randint(ks[9], (B,), 0, 475).astype(jnp.int32)
        return dict(x=x, Wq=Wq, Wk=Wk, Wv=Wv, Wo=Wo, q_norm_w=q_norm_w, k_norm_w=k_norm_w, k_cache=k_cache, v_cache=v_cache, block_table=block_table, cache_seqlens=cache_seqlens)
    _L3_cond_all = _L3_cond_setup()
    _L3_cond_in = {k: v for k, v in _L3_cond_all.items() if k in ('Wq', 'Wk', 'Wv', 'Wo', 'q_norm_w', 'k_norm_w', 'k_cache', 'v_cache')}
    del _L3_cond_all
    return {'x': x, 'itok_B_3_7': itok_B_3_7, 'itok_B_1_7': itok_B_1_7, 'itok_B_0_23': itok_B_0_23, 'itok_Bx16_0_63': itok_Bx16_0_63, 'itok_B_207_1644': itok_B_207_1644, 'L0_cond_weight': _L0_cond_in['weight'], 'L1_cond_weight': _L1_cond_in['weight'], 'L1_cond_bias': _L1_cond_in['bias'], 'L1_cond_lora_a_weights': _L1_cond_in['lora_a_weights'], 'L1_cond_lora_b_weights': _L1_cond_in['lora_b_weights'], 'L1_cond_scaling_factors': _L1_cond_in['scaling_factors'], 'L2_cond_W': _L2_cond_in['W'], 'L2_cond_b': _L2_cond_in['b'], 'L2_cond_lora_As': _L2_cond_in['lora_As'], 'L2_cond_lora_Bs': _L2_cond_in['lora_Bs'], 'L3_cond_Wq': _L3_cond_in['Wq'], 'L3_cond_Wk': _L3_cond_in['Wk'], 'L3_cond_Wv': _L3_cond_in['Wv'], 'L3_cond_Wo': _L3_cond_in['Wo'], 'L3_cond_q_norm_w': _L3_cond_in['q_norm_w'], 'L3_cond_k_norm_w': _L3_cond_in['k_norm_w'], 'L3_cond_k_cache': _L3_cond_in['k_cache'], 'L3_cond_v_cache': _L3_cond_in['v_cache']}

def reference(x, itok_B_3_7, itok_B_1_7, itok_B_0_23, itok_Bx16_0_63, itok_B_207_1644, L0_cond_weight, L1_cond_weight, L1_cond_bias, L1_cond_lora_a_weights, L1_cond_lora_b_weights, L1_cond_scaling_factors, L2_cond_W, L2_cond_b, L2_cond_lora_As, L2_cond_lora_Bs, L3_cond_Wq, L3_cond_Wk, L3_cond_Wv, L3_cond_Wo, L3_cond_q_norm_w, L3_cond_k_norm_w, L3_cond_k_cache, L3_cond_v_cache):
    import jax
    import jax.numpy as jnp

    def _L0_cond_ref(x, weight, adapter_ids):
        import jax, jax.numpy as jnp
        import numpy as np
        MAX_LORAS, OUT, IN = (8, 512, 512)
        B, S = (4, 256)
        w = weight[adapter_ids]
        return jnp.einsum('bsi,boi->bso', x, w)

    def _L1_cond_ref(x, weight, bias, lora_a_weights, lora_b_weights, scaling_factors, adapter_id):
        import jax, jax.numpy as jnp
        import numpy as np
        B, S, D_IN, D_OUT = (4, 256, 512, 512)
        N_ADAPTERS, MAX_RANK = (8, 16)
        base = jnp.einsum('bsi,oi->bso', x, weight) + bias
        a_sel = lora_a_weights[adapter_id]
        b_sel = lora_b_weights[adapter_id]
        scale = scaling_factors[adapter_id]
        low = jnp.einsum('bsi,bri->bsr', x, a_sel)
        delta = jnp.einsum('bsr,bor->bso', low, b_sel)
        return base + scale[:, None, None] * delta

    def _L2_cond_ref(x, adapter_mapping, W, b, lora_As, lora_Bs):
        import jax, jax.numpy as jnp
        import numpy as np
        R = 16
        ALPHA = 32
        SCALING = ALPHA / R
        SLOTS = 32
        IN_F = 512
        OUT_F = 512
        B, T = (8, 128)
        base_out = jnp.einsum('bti,oi->bto', x, W) + b
        A = lora_As[adapter_mapping]
        Bm = lora_Bs[adapter_mapping]
        lora_h = jnp.einsum('bti,bir->btr', x, A)
        lora_out = jnp.einsum('btr,bro->bto', lora_h, Bm)
        return base_out + lora_out * SCALING

    def _L3_cond_ref(x, Wq, Wk, Wv, Wo, q_norm_w, k_norm_w, k_cache, v_cache, block_table, cache_seqlens):
        import jax, jax.numpy as jnp
        import numpy as np
        B, S, HID = (4, 128, 512)
        D, HQ, HK = (128, 32, 8)
        PAGES, PSIZE, NPP = (64, 32, 16)
        THETA = 10000.0
        EPS = 1e-06
        SCALE = 1.0 / float(np.sqrt(D))

        def _rmsnorm(t, w):
            var = jnp.mean(t * t, axis=-1, keepdims=True)
            return t * jax.lax.rsqrt(var + EPS) * w

        def _rope(t, pos):
            inv_freq = 1.0 / THETA ** (jnp.arange(0, D, 2, dtype=jnp.float32) / D)
            freqs = pos[..., None].astype(jnp.float32) * inv_freq
            cos = jnp.cos(freqs)[:, :, None, :]
            sin = jnp.sin(freqs)[:, :, None, :]
            t1, t2 = (t[..., :D // 2], t[..., D // 2:])
            return jnp.concatenate([t1 * cos - t2 * sin, t2 * cos + t1 * sin], axis=-1)
        bsz, seqlen, _ = x.shape
        q = jnp.einsum('bsd,ed->bse', x, Wq).reshape(bsz, seqlen, HQ, D)
        k = jnp.einsum('bsd,ed->bse', x, Wk).reshape(bsz, seqlen, HK, D)
        v = jnp.einsum('bsd,ed->bse', x, Wv).reshape(bsz, seqlen, HK, D)
        q = _rmsnorm(q, q_norm_w)
        k = _rmsnorm(k, k_norm_w)
        pos = cache_seqlens[:, None] + jnp.arange(seqlen)[None, :]
        q = _rope(q, pos)
        k = _rope(k, pos)
        L = NPP * PSIZE
        kc = k_cache[block_table].reshape(bsz, L, HK, D)
        vc = v_cache[block_table].reshape(bsz, L, HK, D)
        k_all = jnp.concatenate([kc, k], axis=1)
        v_all = jnp.concatenate([vc, v], axis=1)
        valid_c = jnp.arange(L)[None, :] < cache_seqlens[:, None]
        valid = jnp.concatenate([valid_c, jnp.ones((bsz, seqlen), dtype=bool)], axis=1)
        rep = HQ // HK
        k_all = jnp.repeat(k_all, rep, axis=2)
        v_all = jnp.repeat(v_all, rep, axis=2)
        scores = jnp.einsum('bqhd,bkhd->bhqk', q, k_all) * SCALE
        scores = jnp.where(valid[:, None, None, :], scores, -1e+30)
        probs = jax.nn.softmax(scores, axis=-1)
        o = jnp.einsum('bhqk,bkhd->bqhd', probs, v_all)
        o = o.reshape(bsz, seqlen, HQ * D)
        return jnp.einsum('bse,de->bsd', o, Wo)
    x = x + _L0_cond_ref(x, L0_cond_weight, itok_B_3_7)
    x = x + _L1_cond_ref(x, L1_cond_weight, L1_cond_bias, L1_cond_lora_a_weights, L1_cond_lora_b_weights, L1_cond_scaling_factors, itok_B_1_7)
    x = x + _L2_cond_ref(x, itok_B_0_23, L2_cond_W, L2_cond_b, L2_cond_lora_As, L2_cond_lora_Bs)
    x = x + _L3_cond_ref(x, L3_cond_Wq, L3_cond_Wk, L3_cond_Wv, L3_cond_Wo, L3_cond_q_norm_w, L3_cond_k_norm_w, L3_cond_k_cache, L3_cond_v_cache, itok_Bx16_0_63, itok_B_207_1644)
    return x

_drawn_inputs = setup_inputs


def setup_inputs(seed=0):
    import zlib

    import numpy as np

    out = dict(_drawn_inputs(seed))
    spreads = {}
    factors = {'L1_cond_bias': 8.0,
     'L2_cond_b': 5.437,
     'L3_cond_Wk': 31.878,
     'L3_cond_Wv': 43.034,
     'L3_cond_q_norm_w': 4.447,
     'L3_cond_k_norm_w': 38.097,
     'L3_cond_k_cache': 8.0,
     'L3_cond_v_cache': 8.0}
    for name, (base, spread) in spreads.items():
        noise = np.random.default_rng([zlib.crc32(name.encode()), seed]).standard_normal(out[name].shape)
        drawn = base * np.exp(spread * noise) if base else spread * noise
        out[name] = jnp.asarray(drawn.astype(out[name].dtype))
    for name, factor in factors.items():
        out[name] = (out[name] * factor).astype(out[name].dtype)
    return out
```

```python
from contextlib import ExitStack

import numpy as np

import concourse.bass as bass
from concourse import mybir

fp32 = mybir.dt.float32
fp32r = mybir.dt.float32r
i32 = mybir.dt.int32
ALU = mybir.AluOpType
ACT = mybir.ActivationFunctionType
AX = mybir.AxisListType

P = 128
NSEQ, SEQ, D = 64, 32, 512
TOK = NSEQ * SEQ
NT = TOK // P
SPT = P // SEQ
KC = D // P
NAD0 = 8
NAD1, NAD2, RANK = 8, 32, 16
DH, HQ, HK = 128, 32, 8
REP = HQ // HK
NPAGE, PSIZE, NPP = 64, 32, 16
NKEY = NPP * PSIZE
NALL = NKEY + SEQ
EPS = 1e-6
SM_SCALE = 1.0 / float(np.sqrt(DH))
MASKED = -1e30
DIAG = D + SEQ


def f32(ap):
    return ap.bitcast(fp32)


class Mem:

    def __init__(self, nc, ctx, tag):
        self.nc, self.ctx, self.tag = nc, ctx, tag

    def sb(self, name, shape, dt=fp32):
        return self.ctx.enter_context(self.nc.sbuf_tensor(f"{self.tag}_{name}", shape, dt))

    def ps(self, name, shape):
        return self.ctx.enter_context(self.nc.psum_tensor(f"{self.tag}_{name}", shape, fp32))

    def sem(self, name):
        return self.ctx.enter_context(self.nc.semaphore(f"{self.tag}_{name}"))

    def sems(self, name, n):
        return [self.sem(f"{name}{i}") for i in range(n)]


def make_identity(pool, ident, zeroed, ready):
    pool.memset(ident[:, :], 0.0).then_inc(zeroed, 1)
    pool.wait_ge(zeroed, 1)
    pool.affine_select(out=ident[:, :], in_=ident[:, :], compare_op=ALU.not_equal, fill=1.0,
                       base=0, pattern=[[-1, P]], channel_multiplier=1).then_inc(ready, 1)


def three_pass(pe, out, xh, xl, wh, wl, start, stop):
    pe.matmul(out, xh, wh, start=start, stop=False)
    pe.matmul(out, xh, wl, start=False, stop=False)
    return pe.matmul(out, xl, wh, start=False, stop=stop)


def later(t, n):
    return not isinstance(t, int) or t >= n


def in_pairs(eng, n, body):
    body(0, False)
    with eng.Fori(1, n - 1) as i:
        body(i, False)
    body(n - 1, True)


def layer0(nc, x_in, ids, w, x_out):
    with ExitStack() as ctx:
        m = Mem(nc, ctx, "l0")
        ident = m.sb("ident", [P, P])
        ids_sb = m.sb("ids", [1, NSEQ], i32)
        w_stage = m.sb("w_stage", [P, 2, KC, D])
        w_hi = m.sb("w_hi", [P, NAD0, KC, D], fp32r)
        w_lo = m.sb("w_lo", [P, NAD0, KC, D], fp32r)
        x_sb = m.sb("x", [P, 2, D])
        xm_hi = m.sb("xm_hi", [P, 2, SPT * DIAG], fp32r)
        xm_lo = m.sb("xm_lo", [P, 2, SPT * DIAG], fp32r)
        y_sb = m.sb("y", [P, 2, D])
        ps_t = m.ps("ps_t", [P, 2, KC, P])
        ps_y = m.ps("ps_y", [P, 2, D])

        zeroed, ident_ready, xm_zeroed = m.sem("zeroed"), m.sem("ident_ready"), m.sem("xm_zeroed")
        ids_loaded = m.sem("ids_loaded")
        w_loaded = m.sems("w_loaded", 2)
        w_hi_done, w_split = m.sem("w_hi_done"), m.sem("w_split")
        x_loaded = m.sems("x_loaded", 2)
        xt_done = m.sem("xt_done")
        hi_done, split_done = m.sem("hi_done"), m.sem("split_done")
        mm_done = m.sem("mm_done")
        y_ready = m.sem("y_ready")
        y_stored = m.sems("y_stored", 2)

        def diagonal(buf, p):
            v = buf[:, p, :].rearrange("p (s r) -> p s r", r=DIAG)
            return v[:, :, 0:D].rearrange("p s (k c) -> p s k c", k=KC)[:, :, :, 0:SEQ]

        def by_seq(p):
            return ps_t[:, p, :, :].rearrange("p k (s c) -> p s k c", s=SPT)

        with nc.Block() as block:
            @block.sync
            def _(sp):
                sp.dma_start(ids_sb[:, :], ids).then_inc(ids_loaded, 16)
                for p in range(2):
                    sp.dma_start(x_sb[:, p, :], x_in[p * P:(p + 1) * P, :]).then_inc(x_loaded[p], 16)
                for a in range(NAD0):
                    if a >= 2:
                        sp.wait_ge(w_split, a - 1)
                    sp.dma_start(w_stage[:, a % 2, :, :], w[a]).then_inc(w_loaded[a % 2], 16)

                def pair(i, last):
                    for p in range(2):
                        t = 2 * i + p
                        sp.wait_ge(y_ready, t + 1)
                        sp.dma_start(x_out[bass.ds(t * P, P), :], y_sb[:, p, :]).then_inc(y_stored[p], 16)
                        if not last:
                            sp.dma_start(x_sb[:, p, :], x_in[bass.ds((t + 2) * P, P), :])\
                              .then_inc(x_loaded[p], 16)

                in_pairs(sp, NT // 2, pair)
                for p in range(2):
                    sp.wait_ge(y_stored[p], 16 * NT // 2)

            @block.gpsimd
            def _(pool):
                make_identity(pool, ident, zeroed, ident_ready)
                pool.memset(f32(xm_hi[:, :, :]), 0.0).then_inc(xm_zeroed, 1)
                pool.memset(f32(xm_lo[:, :, :]), 0.0).then_inc(xm_zeroed, 1)

            @block.scalar
            def _(act):
                for a in range(NAD0):
                    act.wait_ge(w_loaded[a % 2], 16 * (a // 2 + 1))
                    act.activation(w_hi[:, a, :, :], w_stage[:, a % 2, :, :], ACT.Copy).then_inc(w_hi_done, 1)
                act.wait_ge(xm_zeroed, 2)

                def pair(i, last):
                    for p in range(2):
                        t = 2 * i + p
                        act.wait_ge(xt_done, t + 1)
                        if later(t, 2):
                            act.wait_ge(mm_done, t - 1)
                        act.activation(diagonal(xm_hi, p), by_seq(p), ACT.Copy).then_inc(hi_done, 1)

                in_pairs(act, NT // 2, pair)

            @block.vector
            def _(dve):
                def split_lo(t, p):
                    dve.wait_ge(hi_done, t + 1)
                    dve.tensor_tensor(diagonal(xm_lo, p), by_seq(p), f32(diagonal(xm_hi, p)),
                                      ALU.subtract).then_inc(split_done, 1)

                def add(i, t, p):
                    dve.wait_ge(mm_done, t + 1)
                    if later(t, 2):
                        dve.wait_ge(y_stored[p], 16 * i)
                    dve.tensor_tensor(y_sb[:, p, :], ps_y[:, p, :], x_sb[:, p, :], ALU.add).then_inc(y_ready, 1)

                for a in range(NAD0):
                    dve.wait_ge(w_hi_done, a + 1)
                    dve.tensor_tensor(w_lo[:, a, :, :], w_stage[:, a % 2, :, :], f32(w_hi[:, a, :, :]),
                                      ALU.subtract).then_inc(w_split, 1)
                dve.wait_ge(xm_zeroed, 2)
                split_lo(0, 0)

                def pair(i, last):
                    split_lo(2 * i + 1, 1)
                    add(i, 2 * i, 0)
                    if not last:
                        split_lo(2 * i + 2, 0)
                    add(i, 2 * i + 1, 1)

                in_pairs(dve, NT // 2, pair)

            @block.tensor
            def _(pe):
                def transpose(t, p, n):
                    pe.wait_ge(x_loaded[p], 16 * n)
                    if later(t, 2):
                        pe.wait_ge(split_done, t - 1)
                    for k in range(KC):
                        last = pe.transpose(ps_t[:, p, k, :], x_sb[:, p, k * P:(k + 1) * P], ident[:, :])
                    last.then_inc(xt_done, 1)

                def multiply(t, p, meanwhile):
                    pe.wait_ge(split_done, t + 1)
                    if later(t, 2):
                        pe.wait_ge(y_ready, t - 1)
                    _, adapters = nc.values_load_multi_w_load_instructions(
                        ids_sb[0:1, bass.ds(t * SPT, SPT)], engines=[mybir.EngineType.PE],
                        min_val=0, max_val=NAD0 - 1, skip_runtime_bounds_check_because="ids are adapters")
                    for s, a in enumerate(adapters):
                        if s == SPT - 1:
                            meanwhile()
                        for k in range(KC):
                            at = s * D + k * P
                            last = three_pass(pe, ps_y[:, p, :], xm_hi[:, p, at:at + P], xm_lo[:, p, at:at + P],
                                              w_hi[:, bass.ds(a, 1), k, :], w_lo[:, bass.ds(a, 1), k, :],
                                              start=(s == 0 and k == 0), stop=(s == SPT - 1 and k == KC - 1))
                    last.then_inc(mm_done, 1)

                pe.wait_ge(ident_ready, 1)
                transpose(0, 0, 1)
                pe.wait_ge(ids_loaded, 16)
                pe.wait_ge(w_split, NAD0)

                def pair(i, last):
                    multiply(2 * i, 0, lambda: transpose(2 * i + 1, 1, i + 1))
                    multiply(2 * i + 1, 1, lambda: None if last else transpose(2 * i + 2, 0, i + 2))

                in_pairs(pe, NT // 2, pair)


def lora_layer(nc, tag, n_blk, x_in, w, bias, a_all, b_all, ids, slots, factor, x_out):
    with ExitStack() as ctx:
        m = Mem(nc, ctx, tag)
        ident = m.sb("ident", [P, P])
        w_in, w_hi, w_lo = m.sb("w_in", [P, KC, D]), m.sb("w_hi", [P, KC, D], fp32r), m.sb("w_lo", [P, KC, D], fp32r)
        a_shape, b_shape = [P, KC, n_blk * P], [P, n_blk, D]
        a_in, a_hi, a_lo = m.sb("a_in", a_shape), m.sb("a_hi", a_shape, fp32r), m.sb("a_lo", a_shape, fp32r)
        b_in, b_hi, b_lo = m.sb("b_in", b_shape), m.sb("b_hi", b_shape, fp32r), m.sb("b_lo", b_shape, fp32r)
        bias_sb, ids_sb, ids_f = m.sb("bias", [P, D]), m.sb("ids", [P, NSEQ], i32), m.sb("ids_f", [P, NSEQ])
        slots_sb, factor_sb = m.sb("slots", [P, n_blk]), m.sb("factor", [P, 1])
        mask = m.sb("mask", [P, n_blk, NSEQ])
        x_sb, xb_sb, y_sb = m.sb("x", [P, 2, D]), m.sb("xb", [P, 2, D]), m.sb("y", [P, 2, D])
        xt_hi, xt_lo = m.sb("xt_hi", [P, 2, KC, P], fp32r), m.sb("xt_lo", [P, 2, KC, P], fp32r)
        low = m.sb("low", [P, 2, n_blk, P])
        low_hi, low_lo = m.sb("low_hi", [P, 2, n_blk, P], fp32r), m.sb("low_lo", [P, 2, n_blk, P], fp32r)
        ps_t, ps_low = m.ps("ps_t", [P, 2, KC, P]), m.ps("ps_low", [P, 2, D // P, P])
        ps_y = m.ps("ps_y", [P, 2, D])

        zeroed, ident_ready = m.sem("zeroed"), m.sem("ident_ready")
        w_loaded, small_loaded = m.sems("w_loaded", 3), m.sem("small_loaded")
        w_hi_done, w_split = m.sem("w_hi_done"), m.sem("w_split")
        ids_ready, mask_ready = m.sem("ids_ready"), m.sem("mask_ready")
        x_loaded = m.sems("x_loaded", 2)
        xt_done = m.sem("xt_done")
        xb_ready = m.sem("xb_ready")
        hi_done, split_done = m.sem("hi_done"), m.sem("split_done")
        low_done = m.sem("low_done")
        masked, low_hi_done, low_split = m.sem("masked"), m.sem("low_hi_done"), m.sem("low_split")
        mm_done, y_ready = m.sem("mm_done"), m.sem("y_ready")
        y_stored = m.sems("y_stored", 2)
        weights = [(w_in, w_hi, w_lo, w), (a_in, a_hi, a_lo, a_all), (b_in, b_hi, b_lo, b_all)]
        smalls = [(bias_sb, bias), (ids_sb, ids), (slots_sb, slots), (factor_sb, factor)]

        with nc.Block() as block:
            @block.sync
            def _(sp):
                for p in range(2):
                    sp.dma_start(x_sb[:, p, :], x_in[p * P:(p + 1) * P, :]).then_inc(x_loaded[p], 16)
                for buf, src in smalls:
                    sp.dma_start(buf[:, :], src).then_inc(small_loaded, 16)
                for n, (buf, _, _, src) in enumerate(weights):
                    sp.dma_start(buf[:, :, :], src).then_inc(w_loaded[n], 16)

                def pair(i, last):
                    for p in range(2):
                        t = 2 * i + p
                        if not last:
                            sp.wait_ge(xb_ready, t + 1)
                            sp.dma_start(x_sb[:, p, :], x_in[bass.ds((t + 2) * P, P), :])\
                              .then_inc(x_loaded[p], 16)
                        sp.wait_ge(y_ready, t + 1)
                        sp.dma_start(x_out[bass.ds(t * P, P), :], y_sb[:, p, :]).then_inc(y_stored[p], 16)

                in_pairs(sp, NT // 2, pair)
                for p in range(2):
                    sp.wait_ge(y_stored[p], 16 * NT // 2)

            @block.gpsimd
            def _(pool):
                make_identity(pool, ident, zeroed, ident_ready)
                pool.wait_ge(small_loaded, 16 * len(smalls))

                def pair(i, last):
                    for p in range(2):
                        t = 2 * i + p
                        pool.wait_ge(xt_done, t + 1)
                        if later(t, 2):
                            pool.wait_ge(y_ready, t - 1)
                        pool.tensor_tensor(xb_sb[:, p, :], x_sb[:, p, :], bias_sb[:, :], ALU.add).then_inc(xb_ready, 1)

                in_pairs(pool, NT // 2, pair)

            @block.scalar
            def _(act):
                for n, (buf, hi, _, _) in enumerate(weights):
                    act.wait_ge(w_loaded[n], 16)
                    act.activation(hi[:, :, :], buf[:, :, :], ACT.Copy).then_inc(w_hi_done, 1)

                def split_hi(t, p):
                    act.wait_ge(xt_done, t + 1)
                    if later(t, 2):
                        act.wait_ge(mm_done, t - 1)
                    act.activation(xt_hi[:, p, :, :], ps_t[:, p, :, :], ACT.Copy).then_inc(hi_done, 1)

                def low_hi_part(t, p):
                    act.wait_ge(masked, t + 1)
                    act.activation(low_hi[:, p, :, :], low[:, p, :, :], ACT.Copy).then_inc(low_hi_done, 1)

                split_hi(0, 0)

                def pair(i, last):
                    low_hi_part(2 * i, 0)
                    split_hi(2 * i + 1, 1)
                    low_hi_part(2 * i + 1, 1)
                    if not last:
                        split_hi(2 * i + 2, 0)

                in_pairs(act, NT // 2, pair)

            @block.vector
            def _(dve):
                dve.wait_ge(small_loaded, 16 * len(smalls))
                dve.tensor_copy(ids_f[:, :], ids_sb[:, :]).then_inc(ids_ready, 1)
                dve.wait_ge(ids_ready, 1)
                for b in range(n_blk):
                    dve.tensor_scalar(mask[:, b, :], ids_f[:, :], slots_sb[:, b:b + 1], factor_sb[:, 0:1],
                                      ALU.is_equal, ALU.mult).then_inc(mask_ready, 1)
                for n, (buf, hi, lo, _) in enumerate(weights):
                    dve.wait_ge(w_hi_done, n + 1)
                    dve.tensor_tensor(lo[:, :, :], buf[:, :, :], f32(hi[:, :, :]), ALU.subtract).then_inc(w_split, 1)
                dve.wait_ge(mask_ready, n_blk)

                def split_lo(t, p):
                    dve.wait_ge(hi_done, t + 1)
                    dve.tensor_tensor(xt_lo[:, p, :, :], ps_t[:, p, :, :], f32(xt_hi[:, p, :, :]),
                                      ALU.subtract).then_inc(split_done, 1)

                def apply_mask(t, p):
                    dve.wait_ge(low_done, t + 1)
                    keep = mask[:, :, bass.ds(t * SPT, SPT)].unsqueeze(3).to_broadcast([P, n_blk, SPT, SEQ])
                    dve.tensor_tensor(low[:, p, :, :].rearrange("p b (s c) -> p b s c", s=SPT),
                                      ps_low[:, p, 0:n_blk, :].rearrange("p b (s c) -> p b s c", s=SPT),
                                      keep, ALU.mult).then_inc(masked, 1)

                def low_lo_part(t, p):
                    dve.wait_ge(low_hi_done, t + 1)
                    if later(t, 2):
                        dve.wait_ge(mm_done, t - 1)
                    dve.tensor_tensor(low_lo[:, p, :, :], low[:, p, :, :], f32(low_hi[:, p, :, :]),
                                      ALU.subtract).then_inc(low_split, 1)

                def add(i, t, p):
                    dve.wait_ge(mm_done, t + 1)
                    dve.wait_ge(xb_ready, t + 1)
                    if later(t, 2):
                        dve.wait_ge(y_stored[p], 16 * i)
                    dve.tensor_tensor(y_sb[:, p, :], ps_y[:, p, :], xb_sb[:, p, :], ALU.add).then_inc(y_ready, 1)

                split_lo(0, 0)

                def pair(i, last):
                    apply_mask(2 * i, 0)
                    low_lo_part(2 * i, 0)
                    split_lo(2 * i + 1, 1)
                    add(i, 2 * i, 0)
                    apply_mask(2 * i + 1, 1)
                    low_lo_part(2 * i + 1, 1)
                    if not last:
                        split_lo(2 * i + 2, 0)
                    add(i, 2 * i + 1, 1)

                in_pairs(dve, NT // 2, pair)

            @block.tensor
            def _(pe):
                def transpose(t, p, n):
                    pe.wait_ge(x_loaded[p], 16 * n)
                    if later(t, 2):
                        pe.wait_ge(split_done, t - 1)
                    for k in range(KC):
                        last = pe.transpose(ps_t[:, p, k, :], x_sb[:, p, k * P:(k + 1) * P], ident[:, :])
                    last.then_inc(xt_done, 1)

                def low_rank(t, p):
                    pe.wait_ge(split_done, t + 1)
                    if later(t, 2):
                        pe.wait_ge(masked, t - 1)
                    for b in range(n_blk):
                        at = slice(b * P, (b + 1) * P)
                        for k in range(KC):
                            last = three_pass(pe, ps_low[:, p, b, :], a_hi[:, k, at], a_lo[:, k, at],
                                              xt_hi[:, p, k, :], xt_lo[:, p, k, :], k == 0, k == KC - 1)
                    last.then_inc(low_done, 1)

                def base(t, p):
                    if later(t, 2):
                        pe.wait_ge(y_ready, t - 1)
                    for k in range(KC):
                        three_pass(pe, ps_y[:, p, :], xt_hi[:, p, k, :], xt_lo[:, p, k, :],
                                   w_hi[:, k, :], w_lo[:, k, :], k == 0, False)

                def delta(t, p):
                    pe.wait_ge(low_split, t + 1)
                    for b in range(n_blk):
                        last = three_pass(pe, ps_y[:, p, :], low_hi[:, p, b, :], low_lo[:, p, b, :],
                                          b_hi[:, b, :], b_lo[:, b, :], False, b == n_blk - 1)
                    last.then_inc(mm_done, 1)

                pe.wait_ge(ident_ready, 1)
                transpose(0, 0, 1)
                pe.wait_ge(w_split, len(weights))

                def pair(i, last):
                    for p in range(2):
                        t = 2 * i + p
                        low_rank(t, p)
                        if not (last and p):
                            transpose(t + 1, 1 - p, i + 1 + p)
                        base(t, p)
                        delta(t, p)

                in_pairs(pe, NT // 2, pair)


W3 = 2 * (HQ + 2 * HK) * DH // (2 * D)
STEPS = 2 * NT
TWO_PI = 2 * np.pi
PI_HI = 6.28125
PI_MID = round((TWO_PI - PI_HI) * 2 ** 21) / 2 ** 21
PI_LO = TWO_PI - PI_HI - PI_MID
ROUND = 1.5 * 2.0 ** 23
PI_MAX = float(np.float32(3.1415925))


def qkv(nc, x_in, w_all, lens, inv_freq, step_pos, norm_w, q_t, k_t, v_own):
    H = DH // 2
    NB = W3 // 2
    with ExitStack() as ctx:
        m = Mem(nc, ctx, "qkv")
        ident = m.sb("ident", [P, P])
        eps_sb = m.sb("eps", [P, 1])
        x_sb = m.sb("x", [P, 2, D])
        xt_hi, xt_lo = m.sb("xt_hi", [P, KC, TOK], fp32r), m.sb("xt_lo", [P, KC, TOK], fp32r)
        w_stage = m.sb("w_stage", [P, 2, KC, D])
        w_hi, w_lo = m.sb("w_hi", [P, 2, KC, D], fp32r), m.sb("w_lo", [P, 2, KC, D], fp32r)
        lens_sb, pos = m.sb("lens", [P, NT], i32), m.sb("pos", [P, NT])
        freq_sb, step_sb, norm_sb = m.sb("freq", [P, H]), m.sb("step", [P, 1]), m.sb("norm", [P, 2, DH])
        angle, turns, wrapped = m.sb("angle", [P, NT, H]), m.sb("turns", [P, NT, H]), m.sb("wrapped", [P, 2, NT, H])
        sincos = m.sb("sincos", [P, 2, NT, H])
        same, cross = m.sb("same", [P, 2, NT, DH]), m.sb("cross", [P, 2, NT, DH])
        squares, sumsq = m.sb("squares", [P, 2, 4, DH]), m.sb("sumsq", [P, 2, 4])
        rms, inv_rms = m.sb("rms", [P, 2, 4]), m.sb("inv_rms", [P, 2, 4])
        normed = m.sb("normed", [P, 2, 4, DH])
        part_a, part_b = m.sb("part_a", [P, 2, 4, DH]), m.sb("part_b", [P, 2, 4, DH])
        rotated = m.sb("rotated", [P, 2, 4, DH])
        out_t = m.sb("out_t", [P, 2, SPT, 4, SEQ])
        v_sb = m.sb("v", [P, 2, D])
        ps_y, ps_t = m.ps("ps_y", [P, 4, 4, DH]), m.ps("ps_t", [P, 2, 4, P])

        zeroed, ident_ready = m.sem("zeroed"), m.sem("ident_ready")
        x_loaded, xt_done, xhi_done, xt_split = m.sems("x_loaded", 2), m.sem("xt_done"), m.sem("xhi_done"), m.sem("xt_split")
        small_loaded, chain, table_chain, tables = m.sem("small_loaded"), m.sem("chain"), m.sem("table_chain"), m.sem("tables")
        angles_ready, sincos_ready = m.sem("angles_ready"), m.sem("sincos_ready")
        w_loaded, w_hi_done, w_split = m.sems("w_loaded", 2), m.sem("w_hi_done"), m.sem("w_split")
        v_mm_done, v_ready, v_stored = m.sem("v_mm_done"), m.sem("v_ready"), m.sems("v_stored", 2)
        mm_done = m.sem("mm_done")
        squared, summed, rooted, inverted = m.sem("squared"), m.sem("summed"), m.sem("rooted"), m.sem("inverted")
        normed_ready, a_ready, b_ready, rotated_ready = m.sem("normed_ready"), m.sem("a_ready"), m.sem("b_ready"), m.sem("rotated_ready")
        turned, out_ready, stored = m.sem("turned"), m.sem("out_ready"), m.sems("stored", 2)
        smalls = [(lens_sb, lens), (freq_sb, inv_freq), (step_sb, step_pos)]

        def chunk_pairs(eng, body):
            body(0)
            body(1)
            with eng.Fori(2, NB - 1) as b:
                body(b)
            body(NB - 1)

        def is_last(b):
            return isinstance(b, int) and b == NB - 1

        def qk_steps(b, lag, step):
            for j in range(-lag, STEPS if is_last(b) else STEPS - lag):
                if j >= 0:
                    step(STEPS * (b - 1) + j, j, int(is_last(b)))
                elif not (isinstance(b, int) and b == 1):
                    step(STEPS * (b - 1) + j, j + STEPS, 0)

        with nc.Block() as block:
            @block.sync
            def _(sp):
                for p in range(2):
                    sp.dma_start(x_sb[:, p, :], x_in[p * P:(p + 1) * P, :]).then_inc(x_loaded[p], 16)
                for buf, src in smalls:
                    sp.dma_start(buf[:, :], src).then_inc(small_loaded, 16)
                sp.dma_start(norm_sb[:, :, :], norm_w).then_inc(small_loaded, 16)
                for c in range(2):
                    sp.dma_start(w_stage[:, c, :, :], w_all[c]).then_inc(w_loaded[c], 16)

                def x_pair(i, last):
                    for p in range(2):
                        sp.wait_ge(xt_done, 2 * i + p + 1)
                        if not last:
                            sp.dma_start(x_sb[:, p, :], x_in[bass.ds((2 * i + p + 2) * P, P), :])\
                              .then_inc(x_loaded[p], 16)

                in_pairs(sp, NT // 2, x_pair)

                def next_weights(b, c):
                    sp.wait_ge(w_split, 2 * b + c + 1)
                    sp.dma_start(w_stage[:, c, :, :], w_all[bass.ds(2 * b + 2 + c, 1)]).then_inc(w_loaded[c], 16)

                def store(b, j, n, which, c):
                    p, t = j % 2, j % NT
                    sp.wait_ge(out_ready, n + 1)
                    dst = (k_t if which else q_t)[t * SPT:(t + 1) * SPT, :, bass.ds(c, 1), :]
                    sp.dma_start(dst.rearrange("s d c x -> d s (c x)"),
                                 out_t[:, p, :, :, :].rearrange("p s h q -> p s (h q)")).then_inc(stored[p], 16)

                def pair(b):
                    for j in range(STEPS):
                        p, t = j % 2, j % NT
                        if j == 0:
                            next_weights(b, 0) if not is_last(b) else None
                        if j == NT:
                            next_weights(b, 1) if not is_last(b) else None
                        if isinstance(b, int) and b == 0:
                            sp.wait_ge(v_ready, j + 1)
                            c = j // NT
                            sp.dma_start(v_own[t * P:(t + 1) * P, c * D:(c + 1) * D], v_sb[:, p, :])\
                              .then_inc(v_stored[p], 16)
                        else:
                            c = j // NT if is_last(b) else 2 * (b - 1) + j // NT
                            store(b, j, STEPS * (b - 1) + j, int(is_last(b)), c)

                chunk_pairs(sp, pair)
                for p in range(2):
                    sp.wait_ge(v_stored[p], 16 * STEPS // 2)
                    sp.wait_ge(stored[p], 16 * STEPS * (NB - 1) // 2)

            @block.gpsimd
            def _(pool):
                make_identity(pool, ident, zeroed, ident_ready)
                pool.wait_ge(small_loaded, 16 * (len(smalls) + 1))
                pool.wait_ge(sincos_ready, 2)

                def split_lo(g, c):
                    pool.wait_ge(w_hi_done, g + 1)
                    pool.tensor_tensor(w_lo[:, c, :, :], w_stage[:, c, :, :], f32(w_hi[:, c, :, :]),
                                       ALU.subtract).then_inc(w_split, 1)

                split_lo(0, 0)
                split_lo(1, 1)
                for which in range(2):
                    for half in range(2):
                        w_same = norm_sb[:, which:which + 1, half * H:(half + 1) * H].to_broadcast([P, NT, H])
                        w_cross = norm_sb[:, which:which + 1, (1 - half) * H:(2 - half) * H].to_broadcast([P, NT, H])
                        pool.tensor_tensor(same[:, which, :, half * H:(half + 1) * H], sincos[:, 1, :, :], w_same,
                                           ALU.mult).then_inc(tables, 1)
                        pool.tensor_tensor(cross[:, which, :, half * H:(half + 1) * H], sincos[:, 0, :, :], w_cross,
                                           ALU.mult).then_inc(tables, 1)
                pool.wait_ge(tables, 8)
                for which in range(2):
                    pool.tensor_scalar(cross[:, which, :, 0:H], cross[:, which, :, 0:H], -1.0, None, ALU.mult)\
                        .then_inc(tables, 1)

                def rotate(n, j, which):
                    p, t = j % 2, j % NT
                    pool.wait_ge(normed_ready, n + 1)
                    for half in range(2):
                        last = pool.tensor_tensor(
                            part_b[:, p, :, half * H:(half + 1) * H], normed[:, p, :, (1 - half) * H:(2 - half) * H],
                            cross[:, which, t:t + 1, half * H:(half + 1) * H].to_broadcast([P, 4, H]), ALU.mult)
                    last.then_inc(b_ready, 1)
                    pool.wait_ge(a_ready, n + 1)
                    pool.wait_ge(b_ready, n + 1)
                    if later(n, 2):
                        pool.wait_ge(turned, n - 1)
                    pool.tensor_tensor(rotated[:, p, :, :], part_a[:, p, :, :], part_b[:, p, :, :], ALU.add)\
                        .then_inc(rotated_ready, 1)

                def pair(b):
                    if isinstance(b, int) and b == 0:
                        split_lo(2, 0)
                        return
                    def step(n, j, which):
                        if j == 2:
                            split_lo(2 * b + 1, 1)
                        if j == NT + 2 and not is_last(b):
                            split_lo(2 * b + 2, 0)
                        rotate(n, j, which)
                    qk_steps(b, 1, step)

                pool.wait_ge(tables, 10)
                chunk_pairs(pool, pair)

            @block.scalar
            def _(act):
                def split_hi(g, c, n):
                    act.wait_ge(w_loaded[c], 16 * n)
                    if isinstance(g, int) and g in (2, 3):
                        act.wait_ge(v_mm_done, NT * (g - 1))
                    elif later(g, 4):
                        act.wait_ge(mm_done, NT * (g - 3))
                    act.activation(w_hi[:, c, :, :], w_stage[:, c, :, :], ACT.Copy).then_inc(w_hi_done, 1)

                def x_pair(i, last):
                    for p in range(2):
                        t = 2 * i + p
                        act.wait_ge(xt_done, t + 1)
                        act.activation(xt_hi[:, :, bass.ds(t * P, P)], ps_t[:, p, :, :], ACT.Copy)\
                           .then_inc(xhi_done, 1)

                split_hi(0, 0, 1)
                split_hi(1, 1, 1)
                in_pairs(act, NT // 2, x_pair)
                act.wait_ge(angles_ready, 2)
                for a in range(2):
                    act.activation(sincos[:, a, :, :], wrapped[:, a, :, :], ACT.Sin).then_inc(sincos_ready, 1)
                act.wait_ge(tables, 10)

                def square(n, j, which):
                    act.wait_ge(mm_done, n + 1)
                    if later(n, 2):
                        act.wait_ge(summed, n - 1)
                    act.activation(squares[:, j % 2, :, :], ps_y[:, j % 4, :, :], ACT.Square).then_inc(squared, 1)

                def root(n, j, which):
                    act.wait_ge(summed, n + 1)
                    if later(n, 2):
                        act.wait_ge(inverted, n - 1)
                    act.activation(rms[:, j % 2, :], sumsq[:, j % 2, :], ACT.Sqrt, bias=eps_sb[:, 0:1],
                                   scale=1.0 / DH).then_inc(rooted, 1)

                def evacuate(n, j, which, stores):
                    p = j % 2
                    act.wait_ge(turned, n + 1)
                    if later(n, 2):
                        act.wait_ge(stored[p], stores)
                    act.activation(out_t[:, p, :, :, :], ps_t[:, p, :, :].rearrange("p h (s q) -> p s h q", s=SPT),
                                   ACT.Copy).then_inc(out_ready, 1)

                def copy_v(j):
                    act.wait_ge(v_mm_done, j + 1)
                    if j >= 2:
                        act.wait_ge(v_stored[j % 2], 16 * (j // 2))
                    act.activation(v_sb[:, j % 2, :], ps_y[:, j % 4, :, :].rearrange("p h d -> p (h d)"), ACT.Copy)\
                       .then_inc(v_ready, 1)

                def pair(b):
                    if isinstance(b, int) and b == 0:
                        for j in range(STEPS):
                            if j == NT + 2:
                                split_hi(2, 0, 2)
                            copy_v(j)
                        return
                    first = isinstance(b, int) and b == 1
                    flush = 3 if is_last(b) else 0
                    for j in range(STEPS + flush):
                        n = STEPS * (b - 1) + j
                        if j < STEPS:
                            if j == 2:
                                split_hi(2 * b + 1, 1, b + 1)
                            if j == NT + 2 and not is_last(b):
                                split_hi(2 * b + 2, 0, b + 2)
                            square(n, j, 0)
                        if j - 1 < STEPS and not (first and j < 1):
                            root(n - 1, (j - 1) % STEPS, 0)
                        if not (first and j < 3):
                            evacuate(n - 3, (j - 3) % STEPS, 0, 16 * ((STEPS // 2) * (b - 1) + (j - 3) // 2))

                chunk_pairs(act, pair)

            @block.vector
            def _(dve):
                def x_pair(i, last):
                    for p in range(2):
                        t = 2 * i + p
                        dve.wait_ge(xhi_done, t + 1)
                        dve.tensor_tensor(xt_lo[:, :, bass.ds(t * P, P)], ps_t[:, p, :, :],
                                          f32(xt_hi[:, :, bass.ds(t * P, P)]), ALU.subtract).then_inc(xt_split, 1)

                in_pairs(dve, NT // 2, x_pair)
                count = [0]

                def link(instruction):
                    count[0] += 1
                    instruction.then_inc(chain, 1)
                    dve.wait_ge(chain, count[0])

                dve.wait_ge(small_loaded, 16 * (len(smalls) + 1))
                link(dve.memset(eps_sb[:, :], EPS))
                link(dve.tensor_copy(pos[:, :], lens_sb[:, :]))
                link(dve.tensor_scalar(pos[:, :], pos[:, :], step_sb[:, 0:1], None, ALU.add))
                link(dve.tensor_tensor(angle[:, :, :], pos[:, :].unsqueeze(2).to_broadcast([P, NT, H]),
                                       freq_sb[:, :].unsqueeze(1).to_broadcast([P, NT, H]), ALU.mult))
                for a, quarter in ((0, 0.0), (1, 0.25)):
                    r = wrapped[:, a, :, :]
                    link(dve.tensor_scalar(turns[:, :, :], angle[:, :, :], 1.0 / TWO_PI, quarter, ALU.mult, ALU.add))
                    link(dve.tensor_scalar(turns[:, :, :], turns[:, :, :], ROUND, None, ALU.add))
                    link(dve.tensor_scalar(turns[:, :, :], turns[:, :, :], -ROUND, None, ALU.add))
                    link(dve.scalar_tensor_tensor(r, turns[:, :, :], -PI_HI, angle[:, :, :], ALU.mult, ALU.add))
                    link(dve.scalar_tensor_tensor(r, turns[:, :, :], -PI_MID, r, ALU.mult, ALU.add))
                    link(dve.scalar_tensor_tensor(r, turns[:, :, :], -PI_LO, r, ALU.mult, ALU.add))
                    if a:
                        link(dve.tensor_scalar(r, r, float(np.pi / 2), None, ALU.add))
                    dve.tensor_scalar(r, r, PI_MAX, -PI_MAX, ALU.min, ALU.max).then_inc(angles_ready, 1)

                def invert(n, j, which):
                    dve.wait_ge(rooted, n + 1)
                    dve.reciprocal(inv_rms[:, j % 2, :], rms[:, j % 2, :]).then_inc(inverted, 1)

                def add_squares(n, j, which):
                    dve.wait_ge(squared, n + 1)
                    dve.tensor_reduce(sumsq[:, j % 2, :], squares[:, j % 2, :, :], AX.X, ALU.add).then_inc(summed, 1)

                def normalise(n, j, which):
                    p, t = j % 2, j % NT
                    dve.wait_ge(inverted, n + 1)
                    if later(n, 2):
                        dve.wait_ge(rotated_ready, n - 1)
                    dve.tensor_tensor(normed[:, p, :, :], ps_y[:, j % 4, :, :],
                                      inv_rms[:, p, :].unsqueeze(2).to_broadcast([P, 4, DH]), ALU.mult)\
                       .then_inc(normed_ready, 1)
                    dve.wait_ge(normed_ready, n + 1)
                    dve.tensor_tensor(part_a[:, p, :, :], normed[:, p, :, :],
                                      same[:, which, t:t + 1, :].to_broadcast([P, 4, DH]), ALU.mult)\
                       .then_inc(a_ready, 1)

                def pair(b):
                    if isinstance(b, int) and b == 0:
                        return
                    first = isinstance(b, int) and b == 1
                    for j in range(STEPS + (1 if is_last(b) else 0)):
                        n = STEPS * (b - 1) + j
                        before = (n - 1, (j - 1) % STEPS, int(is_last(b) and j > 0))
                        behind = not (first and j < 1)
                        if behind:
                            invert(*before)
                        if j < STEPS:
                            add_squares(n, j, 0)
                        if behind:
                            normalise(*before)

                dve.wait_ge(tables, 10)
                chunk_pairs(dve, pair)

            @block.tensor
            def _(pe):
                pe.wait_ge(ident_ready, 1)

                def x_pair(i, last):
                    for p in range(2):
                        t = 2 * i + p
                        pe.wait_ge(x_loaded[p], 16 * (i + 1))
                        if later(t, 2):
                            pe.wait_ge(xt_split, t - 1)
                        for k in range(KC):
                            last_t = pe.transpose(ps_t[:, p, k, :], x_sb[:, p, k * P:(k + 1) * P], ident[:, :])
                        last_t.then_inc(xt_done, 1)

                in_pairs(pe, NT // 2, x_pair)
                pe.wait_ge(xt_split, NT)

                def multiply(j, done):
                    t, c = j % NT, j // NT
                    for k in range(KC):
                        at = slice(t * P, (t + 1) * P)
                        last = three_pass(pe, ps_y[:, j % 4, :, :].rearrange("p h d -> p (h d)"), xt_hi[:, k, at],
                                          xt_lo[:, k, at], w_hi[:, c, k, :], w_lo[:, c, k, :], k == 0, k == KC - 1)
                    last.then_inc(done, 1)

                def turn(n, j, which):
                    p = j % 2
                    pe.wait_ge(rotated_ready, n + 1)
                    if later(n, 2):
                        pe.wait_ge(out_ready, n - 1)
                    for h in range(4):
                        last = pe.transpose(ps_t[:, p, h, :], rotated[:, p, h, :], ident[:, :])
                    last.then_inc(turned, 1)

                def pair(b):
                    values = isinstance(b, int) and b == 0
                    first = isinstance(b, int) and b == 1
                    for j in range(STEPS + (3 if is_last(b) else 0)):
                        n = STEPS * (b - 1) + j
                        if j < STEPS:
                            if j % NT == 0:
                                pe.wait_ge(w_split, 2 * b + j // NT + 1)
                            if values:
                                if j >= 4:
                                    pe.wait_ge(v_ready, j - 3)
                            elif first and j < 4:
                                pe.wait_ge(v_ready, STEPS - 3 + j)
                            else:
                                pe.wait_ge(normed_ready, n - 3)
                            multiply(j, v_mm_done if values else mm_done)
                        if not values and not (first and j < 3):
                            turn(n - 3, (j - 3) % STEPS, 0)

                chunk_pairs(pe, pair)


UNITS = 2 * HK
OG = 4
K_DMAS, V_DMAS = NPP + 2, NPP + 1


def attention(nc, k_pages, v_pages, table, lens, key_at, q_t, k_own, v_own, o_t):
    with ExitStack() as ctx:
        m = Mem(nc, ctx, "att")
        ident = m.sb("ident", [P, P])
        k_sb = m.sb("k", [P, 2, NPP + 1, HK, PSIZE])
        v_sb, vo_sb = m.sb("v", [P, 2, NPP // 4, HK * DH]), m.sb("vo", [SEQ, 2, HK * DH])
        q_sb = m.sb("q", [P, 2, HK, P])
        lens_sb, lens_f, key_sb = m.sb("lens", [P, NSEQ], i32), m.sb("lens_f", [P, NSEQ]), m.sb("key_at", [P, NKEY])
        mask = m.sb("mask", [P, 2, NALL])
        prob = m.sb("prob", [P, 4, NALL])
        shift, total, inv_total = m.sb("shift", [P, 4]), m.sb("total", [P, 4]), m.sb("inv_total", [P, 4])
        pt_sb, pto_sb = m.sb("pt", [P, 2, NKEY // P, P]), m.sb("pto", [SEQ, 2, P])
        o_sb = m.sb("o", [P, 2, HK, P])
        ps_s = m.ps("ps_s", [P, 2, 2, D])
        ps_pt = m.ps("ps_pt", [P, 2, NKEY // P, P])
        ps_o = m.ps("ps_o", [P, 2, OG, P])

        zeroed, ident_ready = m.sem("zeroed"), m.sem("ident_ready")
        small_loaded, lens_ready, mask_zeroed, mask_ready = m.sem("small_loaded"), m.sem("lens_ready"), m.sem("mask_zeroed"), m.sem("mask_ready")
        k_loaded, v_loaded = m.sems("k_loaded", 2), m.sems("v_loaded", 2)
        s_done = m.sem("s_done")
        masked = m.sem("masked")
        exp_done, inverted, normed = m.sem("exp_done"), m.sem("inverted"), m.sem("normed")
        t_done = m.sem("t_done")
        pt_ready, pto_ready = m.sem("pt_ready"), m.sem("pto_ready")
        pv_done = m.sem("pv_done")
        o_ready, o_stored = m.sem("o_ready"), m.sems("o_stored", 2)

        with nc.Block() as block:
            @block.sync
            def _(sp):
                sp.dma_start(lens_sb[:, :], lens).then_inc(small_loaded, 16)
                sp.dma_start(key_sb[:, :], key_at).then_inc(small_loaded, 16)

                def load(s, p):
                    _, pages = nc.values_load_multi_w_load_instructions(
                        table[bass.ds(s, 1), :], engines=[mybir.EngineType.SP], min_val=0, max_val=NPAGE - 1,
                        skip_runtime_bounds_check_because="block tables name pages")
                    if later(s, 2):
                        sp.wait_ge(s_done, HK * (s - 1))
                    for n, page in enumerate(pages):
                        sp.dma_start(k_sb[:, p, n, :, :].rearrange("p h k -> p (h k)"),
                                     k_pages[bass.ds(page, 1)]).then_inc(k_loaded[p], 16)
                    sp.dma_start(k_sb[:, p, NPP, :, :].rearrange("p h k -> p (h k)"), k_own[bass.ds(s, 1)])\
                      .then_inc(k_loaded[p], 16)
                    sp.dma_start(q_sb[:, p, :, :], q_t[bass.ds(s, 1)]).then_inc(k_loaded[p], 16)
                    if later(s, 2):
                        sp.wait_ge(pv_done, HK * (s - 1))
                    for n, page in enumerate(pages):
                        at = (n % 4) * PSIZE
                        sp.dma_start(v_sb[at:at + PSIZE, p, n // 4, :], v_pages[bass.ds(page, 1)])\
                          .then_inc(v_loaded[p], 16)
                    sp.dma_start(vo_sb[:, p, :], v_own[bass.ds(s * SEQ, SEQ), :]).then_inc(v_loaded[p], 16)

                def store(s, p):
                    sp.wait_ge(o_ready, (HK // OG) * (s + 1))
                    sp.dma_start(o_t[bass.ds(s, 1)], o_sb[:, p, :, :].rearrange("p h q -> p (h q)"))\
                      .then_inc(o_stored[p], 16)

                load(0, 0)
                load(1, 1)

                def pair(i, last):
                    for p in range(2):
                        if not last:
                            load(2 * i + 2 + p, p)
                        store(2 * i + p, p)

                in_pairs(sp, NSEQ // 2, pair)
                for p in range(2):
                    sp.wait_ge(o_stored[p], 16 * NSEQ // 2)

            @block.gpsimd
            def _(pool):
                make_identity(pool, ident, zeroed, ident_ready)
                pool.memset(mask[:, :, NKEY:NALL], 0.0).then_inc(mask_zeroed, 1)

            @block.scalar
            def _(act):
                def exponential(u, j):
                    b = j % 4
                    act.wait_ge(masked, u + 1)
                    act.activation(prob[:, b, :], prob[:, b, :], ACT.Exp, bias=shift[:, b:b + 1], scale=-1.0,
                                   accum_out=total[:, b:b + 1]).then_inc(exp_done, 1)

                def copy_pt(u, j):
                    act.wait_ge(t_done, u + 1)
                    if later(u, 2):
                        act.wait_ge(pv_done, u - 1)
                    act.activation(pt_sb[:, j % 2, :, :], ps_pt[:, j % 2, :, :], ACT.Copy).then_inc(pt_ready, 1)

                def copy_o(i, u, j):
                    p, g = j // HK, j // OG
                    act.wait_ge(pv_done, u + 1)
                    if later(u, UNITS):
                        act.wait_ge(o_stored[p], 16 * i)
                    act.activation(o_sb[:, p, (g % 2) * OG:(g % 2 + 1) * OG, :], ps_o[:, g % 2, :, :], ACT.Copy)\
                       .then_inc(o_ready, 1)

                exponential(0, 0)
                exponential(1, 1)

                def pair(i, last):
                    for j in range(UNITS):
                        u = UNITS * i + j
                        copy_pt(u, j)
                        if not (last and j >= UNITS - 2):
                            exponential(u + 2, (j + 2) % UNITS)
                        if j % OG == 1:
                            if j > 1:
                                copy_o(i, u - 2, j - 2)
                            elif later(u, UNITS):
                                copy_o(i - 1, u - 2, UNITS - 1)
                    if last:
                        copy_o(i, UNITS * i + UNITS - 1, UNITS - 1)

                in_pairs(act, NSEQ // 2, pair)

            @block.vector
            def _(dve):
                dve.wait_ge(small_loaded, 32)
                dve.tensor_copy(lens_f[:, :], lens_sb[:, :]).then_inc(lens_ready, 1)
                dve.wait_ge(lens_ready, 1)
                dve.wait_ge(mask_zeroed, 1)

                def make_mask(s, p):
                    dve.tensor_scalar(mask[:, p, 0:NKEY], key_sb[:, :], lens_f[:, bass.ds(s, 1)], MASKED,
                                      ALU.is_ge, ALU.mult).then_inc(mask_ready, 1)
                    dve.wait_ge(mask_ready, s + 1)

                def wait_for_scores(s, u, j):
                    if j % HK == 0:
                        make_mask(s, j // HK)
                    dve.wait_ge(s_done, u + 1)
                    if later(u, 4):
                        dve.wait_ge(t_done, u - 3)

                def mask_and_max(u, j):
                    b = j % 4
                    dve.tensor_tensor_reduce(
                        out=prob[:, b, :], in0=ps_s[:, j % 2, :, :].rearrange("p a n -> p (a n)")[:, 0:NALL],
                        in1=mask[:, j // HK, :], scale=-SM_SCALE, scalar=3e38, op0=ALU.add, op1=ALU.min,
                        accum_out=shift[:, b:b + 1]).then_inc(masked, 1)

                def invert(u, j):
                    dve.wait_ge(exp_done, u + 1)
                    dve.reciprocal(inv_total[:, j % 4:j % 4 + 1], total[:, j % 4:j % 4 + 1]).then_inc(inverted, 1)

                def normalise(u, j):
                    b = j % 4
                    dve.wait_ge(inverted, u + 1)
                    dve.tensor_scalar(prob[:, b, :], prob[:, b, :], inv_total[:, b:b + 1], None, ALU.mult)\
                       .then_inc(normed, 1)

                def copy_own(u, j):
                    dve.wait_ge(t_done, u + 1)
                    if later(u, 2):
                        dve.wait_ge(pv_done, u - 1)
                    dve.tensor_copy(pto_sb[:, j % 2, :], ps_s[0:SEQ, (j + 1) % 2, 1, P:2 * P]).then_inc(pto_ready, 1)

                for j in range(2):
                    wait_for_scores(0, j, j)
                    mask_and_max(j, j)
                invert(0, 0)
                normalise(0, 0)

                def pair(i, last):
                    for j in range(UNITS):
                        u = UNITS * i + j
                        if not (last and j >= UNITS - 2):
                            wait_for_scores(2 * i + (j + 2) // HK, u + 2, (j + 2) % UNITS)
                        if not (last and j >= UNITS - 1):
                            invert(u + 1, j + 1)
                        if not (last and j >= UNITS - 2):
                            mask_and_max(u + 2, (j + 2) % UNITS)
                        if not (last and j >= UNITS - 1):
                            normalise(u + 1, j + 1)
                        copy_own(u, j)

                in_pairs(dve, NSEQ // 2, pair)

            @block.tensor
            def _(pe):
                def scores(i, u, j):
                    p, h = j // HK, j % HK
                    if h == 0:
                        pe.wait_ge(k_loaded[p], 16 * K_DMAS * (i + 1))
                    if later(u, 2):
                        pe.wait_ge(masked, u - 1)
                    if later(u, 3):
                        pe.wait_ge(pto_ready, u - 2)
                    pe.matmul(ps_s[:, j % 2, 0, :], q_sb[:, p, h, :], k_sb[:, p, 0:NPP, h, :], start=True, stop=True)
                    pe.matmul(ps_s[:, j % 2, 1, 0:SEQ], q_sb[:, p, h, :], k_sb[:, p, NPP, h, :],
                              start=True, stop=True).then_inc(s_done, 1)

                def transpose(u, j):
                    pe.wait_ge(normed, u + 1)
                    if later(u, 2):
                        pe.wait_ge(pt_ready, u - 1)
                    for c in range(NKEY // P):
                        pe.transpose(ps_pt[:, j % 2, c, :], prob[:, j % 4, c * P:(c + 1) * P], ident[:, :])
                    pe.transpose(ps_s[0:SEQ, (j + 1) % 2, 1, P:2 * P], prob[:, j % 4, NKEY:NALL], ident[:, :])\
                      .then_inc(t_done, 1)

                def outputs(i, u, j):
                    p, h, g = j // HK, j % HK, j // OG
                    if h == 0:
                        pe.wait_ge(v_loaded[p], 16 * V_DMAS * (i + 1))
                    if j % OG == 0 and later(u, 2 * OG):
                        pe.wait_ge(o_ready, (UNITS // OG) * i + g - 1)
                    pe.wait_ge(pt_ready, u + 1)
                    out = ps_o[:, g % 2, j % OG, :]
                    for c in range(NKEY // P):
                        pe.matmul(out, v_sb[:, p, c, h * DH:(h + 1) * DH], pt_sb[:, j % 2, c, :],
                                  start=(c == 0), stop=False)
                    pe.wait_ge(pto_ready, u + 1)
                    pe.matmul(out, vo_sb[:, p, h * DH:(h + 1) * DH], pto_sb[:, j % 2, :],
                              start=False, stop=True).then_inc(pv_done, 1)

                pe.wait_ge(ident_ready, 1)
                scores(0, 0, 0)
                scores(0, 1, 1)

                def pair(i, last):
                    for j in range(UNITS):
                        u = UNITS * i + j
                        if not (last and j >= UNITS - 2):
                            scores(i + (j + 2) // UNITS, u + 2, (j + 2) % UNITS)
                        transpose(u, j)
                        if j > 0:
                            outputs(i, u - 1, j - 1)
                        elif later(u, 1):
                            outputs(i - 1, u - 1, UNITS - 1)
                    if last:
                        outputs(i, UNITS * i + UNITS - 1, UNITS - 1)

                in_pairs(pe, NSEQ // 2, pair)


def output_projection(nc, x_in, o_t, w, x_out):
    HH = HQ // 2
    WG = 8
    with ExitStack() as ctx:
        m = Mem(nc, ctx, "out")
        w_stage = m.sb("w_stage", [P, WG, D])
        w_hi, w_lo = m.sb("w_hi", [P, HQ, D], fp32r), m.sb("w_lo", [P, HQ, D], fp32r)
        o_sb = m.sb("o", [P, SPT, HH, SEQ])
        oh_sb, ol_sb = m.sb("o_hi", [P, 2, HH, P], fp32r), m.sb("o_lo", [P, 2, HH, P], fp32r)
        x_sb, y_sb = m.sb("x", [P, D]), m.sb("y", [P, D])
        ps_y = m.ps("ps_y", [P, 2, D])

        w_loaded, w_hi_done, w_split = m.sem("w_loaded"), m.sem("w_hi_done"), m.sem("w_split")
        o_loaded, x_loaded = m.sem("o_loaded"), m.sem("x_loaded")
        hi_done, split_done = m.sem("hi_done"), m.sem("split_done")
        half_done = m.sem("half_done")
        y_ready, y_stored = m.sem("y_ready"), m.sem("y_stored")

        with nc.Block() as block:
            @block.sync
            def _(sp):
                def load_o(t, half):
                    sp.dma_start(o_sb[:, :, :, :].rearrange("p s h q -> p s (h q)"),
                                 o_t[bass.ds(t * SPT, SPT), :, half * HH * SEQ:(half + 1) * HH * SEQ]
                                 .rearrange("s d n -> d s n")).then_inc(o_loaded, 16)

                for g in range(HQ // WG):
                    if g:
                        sp.wait_ge(w_split, g)
                    sp.dma_start(w_stage[:, :, :], w[g]).then_inc(w_loaded, 16)
                    if g == 0:
                        load_o(0, 0)
                        sp.dma_start(x_sb[:, :], x_in[0:P, :]).then_inc(x_loaded, 16)

                def pair(i, last):
                    for p in range(2):
                        t = 2 * i + p
                        sp.wait_ge(split_done, 2 * t + 1)
                        load_o(t, 1)
                        sp.wait_ge(split_done, 2 * t + 2)
                        if not (last and p):
                            load_o(t + 1, 0)
                        sp.wait_ge(y_ready, t + 1)
                        sp.dma_start(x_out[bass.ds(t * P, P), :], y_sb[:, :]).then_inc(y_stored, 16)
                        if not (last and p):
                            sp.dma_start(x_sb[:, :], x_in[bass.ds((t + 1) * P, P), :]).then_inc(x_loaded, 16)

                in_pairs(sp, NT // 2, pair)
                sp.wait_ge(y_stored, 16 * NT)

            @block.scalar
            def _(act):
                for g in range(HQ // WG):
                    act.wait_ge(w_loaded, 16 * (g + 1))
                    act.activation(w_hi[:, g * WG:(g + 1) * WG, :], w_stage[:, :, :], ACT.Copy).then_inc(w_hi_done, 1)

                def pair(i, last):
                    for j in range(4):
                        n = 4 * i + j
                        act.wait_ge(o_loaded, 16 * (n + 1))
                        if later(n, 2):
                            act.wait_ge(half_done, n - 1)
                        act.activation(oh_sb[:, j % 2, :, :].rearrange("p h (s q) -> p s h q", s=SPT),
                                       o_sb[:, :, :, :], ACT.Copy).then_inc(hi_done, 1)

                in_pairs(act, NT // 2, pair)

            @block.vector
            def _(dve):
                for g in range(HQ // WG):
                    at = slice(g * WG, (g + 1) * WG)
                    dve.wait_ge(w_hi_done, g + 1)
                    dve.tensor_tensor(w_lo[:, at, :], w_stage[:, :, :], f32(w_hi[:, at, :]), ALU.subtract)\
                       .then_inc(w_split, 1)

                def split_lo(n, p):
                    dve.wait_ge(hi_done, n + 1)
                    dve.tensor_tensor(ol_sb[:, p, :, :].rearrange("p h (s q) -> p s h q", s=SPT), o_sb[:, :, :, :],
                                      f32(oh_sb[:, p, :, :]).rearrange("p h (s q) -> p s h q", s=SPT),
                                      ALU.subtract).then_inc(split_done, 1)

                def add(t, p):
                    dve.wait_ge(half_done, 2 * t + 2)
                    dve.wait_ge(x_loaded, 16 * (t + 1))
                    if later(t, 1):
                        dve.wait_ge(y_stored, 16 * t)
                    dve.tensor_tensor(y_sb[:, :], ps_y[:, p, :], x_sb[:, :], ALU.add).then_inc(y_ready, 1)

                split_lo(0, 0)
                split_lo(1, 1)

                def pair(i, last):
                    for p in range(2):
                        t = 2 * i + p
                        if not (last and p):
                            split_lo(2 * t + 2, 0)
                        add(t, p)
                        if not (last and p):
                            split_lo(2 * t + 3, 1)

                in_pairs(dve, NT // 2, pair)

            @block.tensor
            def _(pe):
                pe.wait_ge(w_split, HQ // WG)

                def pair(i, last):
                    for p in range(2):
                        t = 2 * i + p
                        if later(t, 2):
                            pe.wait_ge(y_ready, t - 1)
                        for half in range(2):
                            pe.wait_ge(split_done, 2 * t + half + 1)
                            for h in range(HH):
                                mm = three_pass(pe, ps_y[:, p, :], oh_sb[:, half, h, :], ol_sb[:, half, h, :],
                                                w_hi[:, half * HH + h, :], w_lo[:, half * HH + h, :],
                                                half == 0 and h == 0, half == 1 and h == HH - 1)
                            mm.then_inc(half_done, 1)

                in_pairs(pe, NT // 2, pair)


def conditioned_stack(nc, i, out):
    def scratch(name, shape):
        return nc.dram_tensor(name, shape, fp32, kind="Internal").ap()

    x1, x2, x3 = scratch("x1", [TOK, D]), scratch("x2", [TOK, D]), scratch("x3", [TOK, D])
    q_t, k_own = scratch("q_t", [NSEQ, DH, HK, REP * SEQ]), scratch("k_own", [NSEQ, DH, 2, 4 * SEQ])
    v_own, o_t = scratch("v_own", [TOK, HK * DH]), scratch("o_t", [NSEQ, DH, HQ * SEQ])
    layer0(nc, i["x"], i["ids0"], i["w0"], x1)
    lora_layer(nc, "l1", 1, x1, i["w1"], i["bias1"], i["a1"], i["b1"], i["ids1"], i["slots1"], i["factor1"], x2)
    lora_layer(nc, "l2", NAD2 * RANK // P, x2, i["w2"], i["bias2"], i["a2"], i["b2"], i["ids2"], i["slots2"],
               i["factor2"], x3)
    qkv(nc, x3, i["w_qkv"], i["lens_tok"], i["inv_freq"], i["step_pos"], i["norm_w"], q_t, k_own, v_own)
    attention(nc, i["k_pages"], i["v_pages"], i["table"], i["lens_all"], i["key_at"], q_t,
              k_own.rearrange("s d c x -> s d (c x)"), v_own, o_t)
    output_projection(nc, x3, o_t, i["wo"], out)


def laid_out(a):
    def chunked(w_t):
        return w_t.reshape(KC, P, -1).transpose(1, 0, 2)

    def everywhere(v):
        return np.broadcast_to(v.reshape(1, -1), (P, v.size))

    lens = a["itok_B_207_1644"]
    w_qkv = np.concatenate([a["L3_cond_Wv"], a["L3_cond_Wq"], a["L3_cond_Wk"]], axis=0)
    return {
        "x": a["x"].reshape(TOK, D),
        "ids0": a["itok_B_3_7"].reshape(1, NSEQ),
        "w0": a["L0_cond_weight"].transpose(0, 2, 1).reshape(NAD0, KC, P, D).transpose(0, 2, 1, 3),
        "w1": chunked(a["L1_cond_weight"].T),
        "bias1": everywhere(a["L1_cond_bias"]),
        "a1": chunked(a["L1_cond_lora_a_weights"].reshape(NAD1 * RANK, D).T),
        "b1": a["L1_cond_lora_b_weights"].transpose(0, 2, 1).reshape(1, P, D).transpose(1, 0, 2),
        "ids1": everywhere(a["itok_B_1_7"]),
        "slots1": (np.arange(P) // RANK).reshape(P, 1).astype(np.float32),
        "factor1": np.repeat(a["L1_cond_scaling_factors"], RANK).reshape(P, 1),
        "w2": chunked(a["L2_cond_W"].T),
        "bias2": everywhere(a["L2_cond_b"]),
        "a2": chunked(a["L2_cond_lora_As"].transpose(1, 0, 2).reshape(D, NAD2 * RANK)),
        "b2": a["L2_cond_lora_Bs"].reshape(NAD2 * RANK // P, P, D).transpose(1, 0, 2),
        "ids2": everywhere(a["itok_B_0_23"]),
        "slots2": (np.arange(NAD2 * RANK) // RANK).reshape(-1, P).T.astype(np.float32),
        "factor2": np.full((P, 1), 32 / RANK, np.float32),
        "w_qkv": w_qkv.reshape(W3, D, KC, P).transpose(0, 3, 2, 1),
        "lens_tok": np.repeat(lens.reshape(NT, SPT), SEQ, axis=1).T,
        "inv_freq": everywhere((1.0 / 10000.0 ** (np.arange(0, DH, 2) / DH)).astype(np.float32)),
        "step_pos": (np.arange(P) % SEQ).astype(np.float32).reshape(P, 1),
        "norm_w": np.broadcast_to(np.stack([a["L3_cond_q_norm_w"], a["L3_cond_k_norm_w"]]), (P, 2, DH)),
        "k_pages": a["L3_cond_k_cache"].transpose(0, 3, 2, 1).reshape(NPAGE, DH, HK * PSIZE),
        "v_pages": a["L3_cond_v_cache"].reshape(NPAGE, PSIZE, HK * DH),
        "table": a["itok_Bx16_0_63"],
        "lens_all": everywhere(lens),
        "key_at": everywhere(np.arange(NKEY).astype(np.float32)),
        "wo": a["L3_cond_Wo"].T.reshape(4, HQ // 4, DH, D).transpose(0, 2, 1, 3),
    }


def kernel(**inputs):
    import concourse.bacc as bacc
    from concourse.bass_utils import run_bass_kernel_spmd

    arrays = {f"in_{name}": np.ascontiguousarray(v)
              for name, v in laid_out({k: np.asarray(v) for k, v in inputs.items()}).items()}
    nc = bacc.Bacc("TRN2", target_bir_lowering=False, num_devices=1)
    aps = {name[3:]: nc.dram_tensor(name, v.shape, mybir.dt.from_np(v.dtype), kind="ExternalInput").ap()
           for name, v in arrays.items()}
    out = nc.dram_tensor("out", (TOK, D), fp32, kind="ExternalOutput").ap()
    conditioned_stack(nc, aps, out)
    r = run_bass_kernel_spmd(nc, [arrays], core_ids=[0])
    return r.results[0]["out"].reshape(NSEQ, SEQ, D)
```

```python
from contextlib import ExitStack

import numpy as np

import concourse.bass as bass
from concourse import mybir

fp32 = mybir.dt.float32
fp32r = mybir.dt.float32r
i32 = mybir.dt.int32
ALU = mybir.AluOpType
ACT = mybir.ActivationFunctionType
AX = mybir.AxisListType

P = 128
NSEQ, SEQ, D = 64, 32, 512
TOK = NSEQ * SEQ
NT = TOK // P
SPT = P // SEQ
KC = D // P
NAD0 = 8
NAD1, NAD2, RANK = 8, 32, 16
DH, HQ, HK = 128, 32, 8
REP = HQ // HK
NPAGE, PSIZE, NPP = 64, 32, 16
NKEY = NPP * PSIZE
NALL = NKEY + SEQ
EPS = 1e-6
SM_SCALE = 1.0 / float(np.sqrt(DH))
MASKED = -1e30
DIAG = D + SEQ


def f32(ap):
    return ap.bitcast(fp32)


class Mem:

    def __init__(self, nc, ctx, tag):
        self.nc, self.ctx, self.tag = nc, ctx, tag

    def sb(self, name, shape, dt=fp32):
        return self.ctx.enter_context(self.nc.sbuf_tensor(f"{self.tag}_{name}", shape, dt))

    def ps(self, name, shape):
        return self.ctx.enter_context(self.nc.psum_tensor(f"{self.tag}_{name}", shape, fp32))

    def sem(self, name):
        return self.ctx.enter_context(self.nc.semaphore(f"{self.tag}_{name}"))

    def sems(self, name, n):
        return [self.sem(f"{name}{i}") for i in range(n)]


def make_identity(pool, ident, zeroed, ready):
    pool.memset(ident[:, :], 0.0).then_inc(zeroed, 1)
    pool.wait_ge(zeroed, 1)
    pool.affine_select(out=ident[:, :], in_=ident[:, :], compare_op=ALU.not_equal, fill=1.0,
                       base=0, pattern=[[-1, P]], channel_multiplier=1).then_inc(ready, 1)


def three_pass(pe, out, xh, xl, wh, wl, start, stop):
    pe.matmul(out, xh, wh, start=start, stop=False)
    pe.matmul(out, xh, wl, start=False, stop=False)
    return pe.matmul(out, xl, wh, start=False, stop=stop)


def later(t, n):
    return not isinstance(t, int) or t >= n


def in_pairs(eng, n, body):
    body(0, False)
    with eng.Fori(1, n - 1) as i:
        body(i, False)
    body(n - 1, True)


def layer0(nc, x_in, ids, w, x_out):
    with ExitStack() as ctx:
        m = Mem(nc, ctx, "l0")
        ident = m.sb("ident", [P, P])
        ids_sb = m.sb("ids", [1, NSEQ], i32)
        w_stage = m.sb("w_stage", [P, 2, KC, D])
        w_hi = m.sb("w_hi", [P, NAD0, KC, D], fp32r)
        w_lo = m.sb("w_lo", [P, NAD0, KC, D], fp32r)
        x_sb = m.sb("x", [P, 2, D])
        xm_hi = m.sb("xm_hi", [P, 2, SPT * DIAG], fp32r)
        xm_lo = m.sb("xm_lo", [P, 2, SPT * DIAG], fp32r)
        y_sb = m.sb("y", [P, 2, D])
        ps_t = m.ps("ps_t", [P, 2, KC, P])
        ps_y = m.ps("ps_y", [P, 2, D])

        zeroed, ident_ready, xm_zeroed = m.sem("zeroed"), m.sem("ident_ready"), m.sem("xm_zeroed")
        ids_loaded = m.sem("ids_loaded")
        w_loaded = m.sems("w_loaded", 2)
        w_hi_done, w_split = m.sem("w_hi_done"), m.sem("w_split")
        x_loaded = m.sems("x_loaded", 2)
        xt_done = m.sem("xt_done")
        hi_done, split_done = m.sem("hi_done"), m.sem("split_done")
        mm_done = m.sem("mm_done")
        y_ready = m.sem("y_ready")
        y_stored = m.sems("y_stored", 2)

        def diagonal(buf, p):
            v = buf[:, p, :].rearrange("p (s r) -> p s r", r=DIAG)
            return v[:, :, 0:D].rearrange("p s (k c) -> p s k c", k=KC)[:, :, :, 0:SEQ]

        def by_seq(p):
            return ps_t[:, p, :, :].rearrange("p k (s c) -> p s k c", s=SPT)

        with nc.Block() as block:
            @block.sync
            def _(sp):
                sp.dma_start(ids_sb[:, :], ids).then_inc(ids_loaded, 16)
                for p in range(2):
                    sp.dma_start(x_sb[:, p, :], x_in[p * P:(p + 1) * P, :]).then_inc(x_loaded[p], 16)
                for a in range(NAD0):
                    if a >= 2:
                        sp.wait_ge(w_split, a - 1)
                    sp.dma_start(w_stage[:, a % 2, :, :], w[a]).then_inc(w_loaded[a % 2], 16)

                def pair(i, last):
                    for p in range(2):
                        t = 2 * i + p
                        sp.wait_ge(y_ready, t + 1)
                        sp.dma_start(x_out[bass.ds(t * P, P), :], y_sb[:, p, :]).then_inc(y_stored[p], 16)
                        if not last:
                            sp.dma_start(x_sb[:, p, :], x_in[bass.ds((t + 2) * P, P), :])\
                              .then_inc(x_loaded[p], 16)

                in_pairs(sp, NT // 2, pair)
                for p in range(2):
                    sp.wait_ge(y_stored[p], 16 * NT // 2)

            @block.gpsimd
            def _(pool):
                make_identity(pool, ident, zeroed, ident_ready)
                pool.memset(f32(xm_hi[:, :, :]), 0.0).then_inc(xm_zeroed, 1)
                pool.memset(f32(xm_lo[:, :, :]), 0.0).then_inc(xm_zeroed, 1)

            @block.scalar
            def _(act):
                for a in range(NAD0):
                    act.wait_ge(w_loaded[a % 2], 16 * (a // 2 + 1))
                    act.activation(w_hi[:, a, :, :], w_stage[:, a % 2, :, :], ACT.Copy).then_inc(w_hi_done, 1)
                act.wait_ge(xm_zeroed, 2)

                def pair(i, last):
                    for p in range(2):
                        t = 2 * i + p
                        act.wait_ge(xt_done, t + 1)
                        if later(t, 2):
                            act.wait_ge(mm_done, t - 1)
                        act.activation(diagonal(xm_hi, p), by_seq(p), ACT.Copy).then_inc(hi_done, 1)

                in_pairs(act, NT // 2, pair)

            @block.vector
            def _(dve):
                def split_lo(t, p):
                    dve.wait_ge(hi_done, t + 1)
                    dve.tensor_tensor(diagonal(xm_lo, p), by_seq(p), f32(diagonal(xm_hi, p)),
                                      ALU.subtract).then_inc(split_done, 1)

                def add(i, t, p):
                    dve.wait_ge(mm_done, t + 1)
                    if later(t, 2):
                        dve.wait_ge(y_stored[p], 16 * i)
                    dve.tensor_tensor(y_sb[:, p, :], ps_y[:, p, :], x_sb[:, p, :], ALU.add).then_inc(y_ready, 1)

                for a in range(NAD0):
                    dve.wait_ge(w_hi_done, a + 1)
                    dve.tensor_tensor(w_lo[:, a, :, :], w_stage[:, a % 2, :, :], f32(w_hi[:, a, :, :]),
                                      ALU.subtract).then_inc(w_split, 1)
                dve.wait_ge(xm_zeroed, 2)
                split_lo(0, 0)

                def pair(i, last):
                    split_lo(2 * i + 1, 1)
                    add(i, 2 * i, 0)
                    if not last:
                        split_lo(2 * i + 2, 0)
                    add(i, 2 * i + 1, 1)

                in_pairs(dve, NT // 2, pair)

            @block.tensor
            def _(pe):
                def transpose(t, p, n):
                    pe.wait_ge(x_loaded[p], 16 * n)
                    if later(t, 2):
                        pe.wait_ge(split_done, t - 1)
                    for k in range(KC):
                        last = pe.transpose(ps_t[:, p, k, :], x_sb[:, p, k * P:(k + 1) * P], ident[:, :])
                    last.then_inc(xt_done, 1)

                def multiply(t, p, meanwhile):
                    pe.wait_ge(split_done, t + 1)
                    if later(t, 2):
                        pe.wait_ge(y_ready, t - 1)
                    _, adapters = nc.values_load_multi_w_load_instructions(
                        ids_sb[0:1, bass.ds(t * SPT, SPT)], engines=[mybir.EngineType.PE],
                        min_val=0, max_val=NAD0 - 1, skip_runtime_bounds_check_because="ids are adapters")
                    for s, a in enumerate(adapters):
                        if s == SPT - 1:
                            meanwhile()
                        for k in range(KC):
                            at = s * D + k * P
                            last = three_pass(pe, ps_y[:, p, :], xm_hi[:, p, at:at + P], xm_lo[:, p, at:at + P],
                                              w_hi[:, bass.ds(a, 1), k, :], w_lo[:, bass.ds(a, 1), k, :],
                                              start=(s == 0 and k == 0), stop=(s == SPT - 1 and k == KC - 1))
                    last.then_inc(mm_done, 1)

                pe.wait_ge(ident_ready, 1)
                transpose(0, 0, 1)
                pe.wait_ge(ids_loaded, 16)
                pe.wait_ge(w_split, NAD0)

                def pair(i, last):
                    multiply(2 * i, 0, lambda: transpose(2 * i + 1, 1, i + 1))
                    multiply(2 * i + 1, 1, lambda: None if last else transpose(2 * i + 2, 0, i + 2))

                in_pairs(pe, NT // 2, pair)


def lora_layer(nc, tag, n_blk, x_in, w, bias, a_all, b_all, ids, slots, factor, x_out):
    with ExitStack() as ctx:
        m = Mem(nc, ctx, tag)
        ident = m.sb("ident", [P, P])
        w_in, w_hi, w_lo = m.sb("w_in", [P, KC, D]), m.sb("w_hi", [P, KC, D], fp32r), m.sb("w_lo", [P, KC, D], fp32r)
        a_shape, b_shape = [P, KC, n_blk * P], [P, n_blk, D]
        a_in, a_hi, a_lo = m.sb("a_in", a_shape), m.sb("a_hi", a_shape, fp32r), m.sb("a_lo", a_shape, fp32r)
        b_in, b_hi, b_lo = m.sb("b_in", b_shape), m.sb("b_hi", b_shape, fp32r), m.sb("b_lo", b_shape, fp32r)
        bias_sb, ids_sb, ids_f = m.sb("bias", [P, D]), m.sb("ids", [P, NSEQ], i32), m.sb("ids_f", [P, NSEQ])
        slots_sb, factor_sb = m.sb("slots", [P, n_blk]), m.sb("factor", [P, 1])
        mask = m.sb("mask", [P, n_blk, NSEQ])
        x_sb, xb_sb, y_sb = m.sb("x", [P, 2, D]), m.sb("xb", [P, 2, D]), m.sb("y", [P, 2, D])
        xt_hi, xt_lo = m.sb("xt_hi", [P, 2, KC, P], fp32r), m.sb("xt_lo", [P, 2, KC, P], fp32r)
        low = m.sb("low", [P, 2, n_blk, P])
        low_hi, low_lo = m.sb("low_hi", [P, 2, n_blk, P], fp32r), m.sb("low_lo", [P, 2, n_blk, P], fp32r)
        ps_t, ps_low = m.ps("ps_t", [P, 2, KC, P]), m.ps("ps_low", [P, 2, D // P, P])
        ps_y = m.ps("ps_y", [P, 2, D])

        zeroed, ident_ready = m.sem("zeroed"), m.sem("ident_ready")
        w_loaded, small_loaded = m.sems("w_loaded", 3), m.sem("small_loaded")
        w_hi_done, w_split = m.sem("w_hi_done"), m.sem("w_split")
        ids_ready, mask_ready = m.sem("ids_ready"), m.sem("mask_ready")
        x_loaded = m.sems("x_loaded", 2)
        xt_done = m.sem("xt_done")
        xb_ready = m.sem("xb_ready")
        hi_done, split_done = m.sem("hi_done"), m.sem("split_done")
        low_done = m.sem("low_done")
        masked, low_hi_done, low_split = m.sem("masked"), m.sem("low_hi_done"), m.sem("low_split")
        mm_done, y_ready = m.sem("mm_done"), m.sem("y_ready")
        y_stored = m.sems("y_stored", 2)
        weights = [(w_in, w_hi, w_lo, w), (a_in, a_hi, a_lo, a_all), (b_in, b_hi, b_lo, b_all)]
        smalls = [(bias_sb, bias), (ids_sb, ids), (slots_sb, slots), (factor_sb, factor)]

        with nc.Block() as block:
            @block.sync
            def _(sp):
                for p in range(2):
                    sp.dma_start(x_sb[:, p, :], x_in[p * P:(p + 1) * P, :]).then_inc(x_loaded[p], 16)
                for buf, src in smalls:
                    sp.dma_start(buf[:, :], src).then_inc(small_loaded, 16)
                for n, (buf, _, _, src) in enumerate(weights):
                    sp.dma_start(buf[:, :, :], src).then_inc(w_loaded[n], 16)

                def pair(i, last):
                    for p in range(2):
                        t = 2 * i + p
                        if not last:
                            sp.wait_ge(xb_ready, t + 1)
                            sp.dma_start(x_sb[:, p, :], x_in[bass.ds((t + 2) * P, P), :])\
                              .then_inc(x_loaded[p], 16)
                        sp.wait_ge(y_ready, t + 1)
                        sp.dma_start(x_out[bass.ds(t * P, P), :], y_sb[:, p, :]).then_inc(y_stored[p], 16)

                in_pairs(sp, NT // 2, pair)
                for p in range(2):
                    sp.wait_ge(y_stored[p], 16 * NT // 2)

            @block.gpsimd
            def _(pool):
                make_identity(pool, ident, zeroed, ident_ready)
                pool.wait_ge(small_loaded, 16 * len(smalls))

                def pair(i, last):
                    for p in range(2):
                        t = 2 * i + p
                        pool.wait_ge(xt_done, t + 1)
                        if later(t, 2):
                            pool.wait_ge(y_ready, t - 1)
                        pool.tensor_tensor(xb_sb[:, p, :], x_sb[:, p, :], bias_sb[:, :], ALU.add).then_inc(xb_ready, 1)

                in_pairs(pool, NT // 2, pair)

            @block.scalar
            def _(act):
                for n, (buf, hi, _, _) in enumerate(weights):
                    act.wait_ge(w_loaded[n], 16)
                    act.activation(hi[:, :, :], buf[:, :, :], ACT.Copy).then_inc(w_hi_done, 1)

                def split_hi(t, p):
                    act.wait_ge(xt_done, t + 1)
                    if later(t, 2):
                        act.wait_ge(mm_done, t - 1)
                    act.activation(xt_hi[:, p, :, :], ps_t[:, p, :, :], ACT.Copy).then_inc(hi_done, 1)

                def low_hi_part(t, p):
                    act.wait_ge(masked, t + 1)
                    act.activation(low_hi[:, p, :, :], low[:, p, :, :], ACT.Copy).then_inc(low_hi_done, 1)

                split_hi(0, 0)

                def pair(i, last):
                    low_hi_part(2 * i, 0)
                    split_hi(2 * i + 1, 1)
                    low_hi_part(2 * i + 1, 1)
                    if not last:
                        split_hi(2 * i + 2, 0)

                in_pairs(act, NT // 2, pair)

            @block.vector
            def _(dve):
                dve.wait_ge(small_loaded, 16 * len(smalls))
                dve.tensor_copy(ids_f[:, :], ids_sb[:, :]).then_inc(ids_ready, 1)
                dve.wait_ge(ids_ready, 1)
                for b in range(n_blk):
                    dve.tensor_scalar(mask[:, b, :], ids_f[:, :], slots_sb[:, b:b + 1], factor_sb[:, 0:1],
                                      ALU.is_equal, ALU.mult).then_inc(mask_ready, 1)
                for n, (buf, hi, lo, _) in enumerate(weights):
                    dve.wait_ge(w_hi_done, n + 1)
                    dve.tensor_tensor(lo[:, :, :], buf[:, :, :], f32(hi[:, :, :]), ALU.subtract).then_inc(w_split, 1)
                dve.wait_ge(mask_ready, n_blk)

                def split_lo(t, p):
                    dve.wait_ge(hi_done, t + 1)
                    dve.tensor_tensor(xt_lo[:, p, :, :], ps_t[:, p, :, :], f32(xt_hi[:, p, :, :]),
                                      ALU.subtract).then_inc(split_done, 1)

                def apply_mask(t, p):
                    dve.wait_ge(low_done, t + 1)
                    keep = mask[:, :, bass.ds(t * SPT, SPT)].unsqueeze(3).to_broadcast([P, n_blk, SPT, SEQ])
                    dve.tensor_tensor(low[:, p, :, :].rearrange("p b (s c) -> p b s c", s=SPT),
                                      ps_low[:, p, 0:n_blk, :].rearrange("p b (s c) -> p b s c", s=SPT),
                                      keep, ALU.mult).then_inc(masked, 1)

                def low_lo_part(t, p):
                    dve.wait_ge(low_hi_done, t + 1)
                    if later(t, 2):
                        dve.wait_ge(mm_done, t - 1)
                    dve.tensor_tensor(low_lo[:, p, :, :], low[:, p, :, :], f32(low_hi[:, p, :, :]),
                                      ALU.subtract).then_inc(low_split, 1)

                def add(i, t, p):
                    dve.wait_ge(mm_done, t + 1)
                    dve.wait_ge(xb_ready, t + 1)
                    if later(t, 2):
                        dve.wait_ge(y_stored[p], 16 * i)
                    dve.tensor_tensor(y_sb[:, p, :], ps_y[:, p, :], xb_sb[:, p, :], ALU.add).then_inc(y_ready, 1)

                split_lo(0, 0)

                def pair(i, last):
                    apply_mask(2 * i, 0)
                    low_lo_part(2 * i, 0)
                    split_lo(2 * i + 1, 1)
                    add(i, 2 * i, 0)
                    apply_mask(2 * i + 1, 1)
                    low_lo_part(2 * i + 1, 1)
                    if not last:
                        split_lo(2 * i + 2, 0)
                    add(i, 2 * i + 1, 1)

                in_pairs(dve, NT // 2, pair)

            @block.tensor
            def _(pe):
                def transpose(t, p, n):
                    pe.wait_ge(x_loaded[p], 16 * n)
                    if later(t, 2):
                        pe.wait_ge(split_done, t - 1)
                    for k in range(KC):
                        last = pe.transpose(ps_t[:, p, k, :], x_sb[:, p, k * P:(k + 1) * P], ident[:, :])
                    last.then_inc(xt_done, 1)

                def low_rank(t, p):
                    pe.wait_ge(split_done, t + 1)
                    if later(t, 2):
                        pe.wait_ge(masked, t - 1)
                    for b in range(n_blk):
                        at = slice(b * P, (b + 1) * P)
                        for k in range(KC):
                            last = three_pass(pe, ps_low[:, p, b, :], a_hi[:, k, at], a_lo[:, k, at],
                                              xt_hi[:, p, k, :], xt_lo[:, p, k, :], k == 0, k == KC - 1)
                    last.then_inc(low_done, 1)

                def base(t, p):
                    if later(t, 2):
                        pe.wait_ge(y_ready, t - 1)
                    for k in range(KC):
                        three_pass(pe, ps_y[:, p, :], xt_hi[:, p, k, :], xt_lo[:, p, k, :],
                                   w_hi[:, k, :], w_lo[:, k, :], k == 0, False)

                def delta(t, p):
                    pe.wait_ge(low_split, t + 1)
                    for b in range(n_blk):
                        last = three_pass(pe, ps_y[:, p, :], low_hi[:, p, b, :], low_lo[:, p, b, :],
                                          b_hi[:, b, :], b_lo[:, b, :], False, b == n_blk - 1)
                    last.then_inc(mm_done, 1)

                pe.wait_ge(ident_ready, 1)
                transpose(0, 0, 1)
                pe.wait_ge(w_split, len(weights))

                def pair(i, last):
                    for p in range(2):
                        t = 2 * i + p
                        low_rank(t, p)
                        if not (last and p):
                            transpose(t + 1, 1 - p, i + 1 + p)
                        base(t, p)
                        delta(t, p)

                in_pairs(pe, NT // 2, pair)


W3 = 2 * (HQ + 2 * HK) * DH // (2 * D)
STEPS = 2 * NT
TWO_PI = 2 * np.pi
PI_HI = 6.28125
PI_MID = round((TWO_PI - PI_HI) * 2 ** 21) / 2 ** 21
PI_LO = TWO_PI - PI_HI - PI_MID
ROUND = 1.5 * 2.0 ** 23
PI_MAX = float(np.float32(3.1415925))


def qkv(nc, x_in, w_all, lens, inv_freq, step_pos, norm_w, q_t, k_t, v_own):
    H = DH // 2
    NB = W3 // 2
    XB = 4
    with ExitStack() as ctx:
        m = Mem(nc, ctx, "qkv")
        ident = m.sb("ident", [P, P])
        eps_sb = m.sb("eps", [P, 1])
        x_sb = m.sb("x", [P, XB, D])
        xt_hi, xt_lo = m.sb("xt_hi", [P, KC, TOK], fp32r), m.sb("xt_lo", [P, KC, TOK], fp32r)
        w_stage = m.sb("w_stage", [P, 2, KC, D])
        w_hi, w_lo = m.sb("w_hi", [P, 2, KC, D], fp32r), m.sb("w_lo", [P, 2, KC, D], fp32r)
        lens_sb, pos = m.sb("lens", [P, NT], i32), m.sb("pos", [P, NT])
        freq_sb, step_sb, norm_sb = m.sb("freq", [P, H]), m.sb("step", [P, 1]), m.sb("norm", [P, 2, DH])
        angle, turns, wrapped = m.sb("angle", [P, NT, H]), m.sb("turns", [P, NT, H]), m.sb("wrapped", [P, 2, NT, H])
        sincos = m.sb("sincos", [P, 2, NT, H])
        same, cross = m.sb("same", [P, 2, NT, DH]), m.sb("cross", [P, 2, NT, DH])
        squares, sumsq = m.sb("squares", [P, 2, 4, DH]), m.sb("sumsq", [P, 2, 4])
        rms, inv_rms = m.sb("rms", [P, 2, 4]), m.sb("inv_rms", [P, 2, 4])
        normed = m.sb("normed", [P, 2, 4, DH])
        part_a, part_b = m.sb("part_a", [P, 2, 4, DH]), m.sb("part_b", [P, 2, 4, DH])
        rotated = m.sb("rotated", [P, 2, 4, DH])
        out_t = m.sb("out_t", [P, 2, SPT, 4, SEQ])
        v_sb = m.sb("v", [P, 2, D])
        ps_y, ps_t = m.ps("ps_y", [P, 4, 4, DH]), m.ps("ps_t", [P, 2, 4, P])

        zeroed, ident_ready = m.sem("zeroed"), m.sem("ident_ready")
        x_loaded, xt_done, xhi_done, xt_split = m.sems("x_loaded", XB), m.sem("xt_done"), m.sem("xhi_done"), m.sem("xt_split")
        small_loaded, chain, table_chain, tables = m.sem("small_loaded"), m.sem("chain"), m.sem("table_chain"), m.sem("tables")
        angles_ready, sincos_ready = m.sem("angles_ready"), m.sem("sincos_ready")
        w_loaded, w_hi_done, w_split = m.sems("w_loaded", 2), m.sem("w_hi_done"), m.sem("w_split")
        v_mm_done, v_ready, v_stored = m.sem("v_mm_done"), m.sem("v_ready"), m.sems("v_stored", 2)
        mm_done = m.sem("mm_done")
        squared, summed, rooted, inverted = m.sem("squared"), m.sem("summed"), m.sem("rooted"), m.sem("inverted")
        normed_ready, a_ready, b_ready, rotated_ready = m.sem("normed_ready"), m.sem("a_ready"), m.sem("b_ready"), m.sem("rotated_ready")
        turned, out_ready, stored = m.sem("turned"), m.sem("out_ready"), m.sems("stored", 2)
        smalls = [(lens_sb, lens), (freq_sb, inv_freq), (step_sb, step_pos)]

        def chunk_pairs(eng, body):
            body(0)
            body(1)
            with eng.Fori(2, NB - 1) as b:
                body(b)
            body(NB - 1)

        def is_last(b):
            return isinstance(b, int) and b == NB - 1

        def qk_steps(b, lag, step):
            for j in range(-lag, STEPS if is_last(b) else STEPS - lag):
                if j >= 0:
                    step(STEPS * (b - 1) + j, j, int(is_last(b)))
                elif not (isinstance(b, int) and b == 1):
                    step(STEPS * (b - 1) + j, j + STEPS, 0)

        with nc.Block() as block:
            @block.sync
            def _(sp):
                def load_x(t):
                    sp.dma_start(x_sb[:, t % XB, :], x_in[t * P:(t + 1) * P, :]).then_inc(x_loaded[t % XB], 16)

                def load_w(c):
                    sp.dma_start(w_stage[:, c, :, :], w_all[c]).then_inc(w_loaded[c], 16)

                load_x(0)
                load_w(0)
                for t in range(1, XB):
                    load_x(t)
                load_w(1)
                for buf, src in smalls:
                    sp.dma_start(buf[:, :], src).then_inc(small_loaded, 16)
                sp.dma_start(norm_sb[:, :, :], norm_w).then_inc(small_loaded, 16)

                def next_weights(b, c):
                    sp.wait_ge(w_split, 2 * b + c + 1)
                    sp.dma_start(w_stage[:, c, :, :], w_all[bass.ds(2 * b + 2 + c, 1)]).then_inc(w_loaded[c], 16)

                def store(b, j, n, which, c):
                    p, t = j % 2, j % NT
                    sp.wait_ge(out_ready, n + 1)
                    dst = (k_t if which else q_t)[t * SPT:(t + 1) * SPT, :, bass.ds(c, 1), :]
                    sp.dma_start(dst.rearrange("s d c x -> d s (c x)"),
                                 out_t[:, p, :, :, :].rearrange("p s h q -> p s (h q)")).then_inc(stored[p], 16)

                def pair(b):
                    for j in range(STEPS):
                        p, t = j % 2, j % NT
                        if j == 0:
                            next_weights(b, 0) if not is_last(b) else None
                        if j == NT:
                            next_weights(b, 1) if not is_last(b) else None
                        if isinstance(b, int) and b == 0:
                            if j + XB < NT:
                                sp.wait_ge(xt_done, j + 1)
                                load_x(j + XB)
                            sp.wait_ge(v_ready, j + 1)
                            c = j // NT
                            sp.dma_start(v_own[t * P:(t + 1) * P, c * D:(c + 1) * D], v_sb[:, p, :])\
                              .then_inc(v_stored[p], 16)
                        else:
                            c = j // NT if is_last(b) else 2 * (b - 1) + j // NT
                            store(b, j, STEPS * (b - 1) + j, int(is_last(b)), c)

                chunk_pairs(sp, pair)
                for p in range(2):
                    sp.wait_ge(v_stored[p], 16 * STEPS // 2)
                    sp.wait_ge(stored[p], 16 * STEPS * (NB - 1) // 2)

            @block.gpsimd
            def _(pool):
                make_identity(pool, ident, zeroed, ident_ready)

                def split_lo(g, c):
                    pool.wait_ge(w_hi_done, g + 1)
                    pool.tensor_tensor(w_lo[:, c, :, :], w_stage[:, c, :, :], f32(w_hi[:, c, :, :]),
                                       ALU.subtract).then_inc(w_split, 1)

                split_lo(0, 0)
                split_lo(1, 1)
                pool.wait_ge(small_loaded, 16 * (len(smalls) + 1))
                pool.wait_ge(sincos_ready, 2)
                for which in range(2):
                    for half in range(2):
                        w_same = norm_sb[:, which:which + 1, half * H:(half + 1) * H].to_broadcast([P, NT, H])
                        w_cross = norm_sb[:, which:which + 1, (1 - half) * H:(2 - half) * H].to_broadcast([P, NT, H])
                        pool.tensor_tensor(same[:, which, :, half * H:(half + 1) * H], sincos[:, 1, :, :], w_same,
                                           ALU.mult).then_inc(tables, 1)
                        pool.tensor_tensor(cross[:, which, :, half * H:(half + 1) * H], sincos[:, 0, :, :], w_cross,
                                           ALU.mult).then_inc(tables, 1)
                pool.wait_ge(tables, 8)
                for which in range(2):
                    pool.tensor_scalar(cross[:, which, :, 0:H], cross[:, which, :, 0:H], -1.0, None, ALU.mult)\
                        .then_inc(tables, 1)

                def cross_part(n, j, which):
                    p, t = j % 2, j % NT
                    pool.wait_ge(normed_ready, n + 1)
                    for half in range(2):
                        last = pool.tensor_tensor(
                            part_b[:, p, :, half * H:(half + 1) * H], normed[:, p, :, (1 - half) * H:(2 - half) * H],
                            cross[:, which, t:t + 1, half * H:(half + 1) * H].to_broadcast([P, 4, H]), ALU.mult)
                    last.then_inc(b_ready, 1)

                def pair(b):
                    if isinstance(b, int) and b == 0:
                        split_lo(2, 0)
                        return
                    def step(n, j, which):
                        if j == 2:
                            split_lo(2 * b + 1, 1)
                        if j == NT + 2 and not is_last(b):
                            split_lo(2 * b + 2, 0)
                        cross_part(n, j, which)
                    qk_steps(b, 1, step)

                pool.wait_ge(tables, 10)
                chunk_pairs(pool, pair)

            @block.scalar
            def _(act):
                def split_hi(g, c, n):
                    act.wait_ge(w_loaded[c], 16 * n)
                    if isinstance(g, int) and g in (2, 3):
                        act.wait_ge(v_mm_done, NT * (g - 1))
                    elif later(g, 4):
                        act.wait_ge(mm_done, NT * (g - 3))
                    act.activation(w_hi[:, c, :, :], w_stage[:, c, :, :], ACT.Copy).then_inc(w_hi_done, 1)

                def x_hi(t):
                    act.wait_ge(xt_done, t + 1)
                    act.activation(xt_hi[:, :, t * P:(t + 1) * P], ps_t[:, t % 2, :, :], ACT.Copy).then_inc(xhi_done, 1)

                x_hi(0)
                split_hi(0, 0, 1)
                x_hi(1)
                split_hi(1, 1, 1)

                def square(n, j, which):
                    act.wait_ge(mm_done, n + 1)
                    if later(n, 2):
                        act.wait_ge(summed, n - 1)
                    act.activation(squares[:, j % 2, :, :], ps_y[:, j % 4, :, :], ACT.Square).then_inc(squared, 1)

                def root(n, j, which):
                    act.wait_ge(summed, n + 1)
                    if later(n, 2):
                        act.wait_ge(inverted, n - 1)
                    act.activation(rms[:, j % 2, :], sumsq[:, j % 2, :], ACT.Sqrt, bias=eps_sb[:, 0:1],
                                   scale=1.0 / DH).then_inc(rooted, 1)

                def evacuate(n, j, which, stores):
                    p = j % 2
                    act.wait_ge(turned, n + 1)
                    if later(n, 2):
                        act.wait_ge(stored[p], stores)
                    act.activation(out_t[:, p, :, :, :], ps_t[:, p, :, :].rearrange("p h (s q) -> p s h q", s=SPT),
                                   ACT.Copy).then_inc(out_ready, 1)

                def copy_v(j):
                    act.wait_ge(v_mm_done, j + 1)
                    if j >= 2:
                        act.wait_ge(v_stored[j % 2], 16 * (j // 2))
                    act.activation(v_sb[:, j % 2, :], ps_y[:, j % 4, :, :].rearrange("p h d -> p (h d)"), ACT.Copy)\
                       .then_inc(v_ready, 1)

                def pair(b):
                    if isinstance(b, int) and b == 0:
                        for j in range(STEPS):
                            if j + 2 < NT:
                                x_hi(j + 2)
                            if j == NT:
                                act.wait_ge(angles_ready, 2)
                                for a in range(2):
                                    act.activation(sincos[:, a, :, :], wrapped[:, a, :, :], ACT.Sin)\
                                       .then_inc(sincos_ready, 1)
                            if j == NT + 2:
                                split_hi(2, 0, 2)
                            copy_v(j)
                        act.wait_ge(tables, 10)
                        return
                    first = isinstance(b, int) and b == 1
                    flush = 3 if is_last(b) else 0
                    for j in range(STEPS + flush):
                        n = STEPS * (b - 1) + j
                        if j < STEPS:
                            if j == 2:
                                split_hi(2 * b + 1, 1, b + 1)
                            if j == NT + 2 and not is_last(b):
                                split_hi(2 * b + 2, 0, b + 2)
                        if j - 1 < STEPS and not (first and j < 1):
                            root(n - 1, (j - 1) % STEPS, 0)
                        if j < STEPS:
                            square(n, j, 0)
                        if not (first and j < 3):
                            evacuate(n - 3, (j - 3) % STEPS, 0, 16 * ((STEPS // 2) * (b - 1) + (j - 3) // 2))

                chunk_pairs(act, pair)

            @block.vector
            def _(dve):
                def x_lo(t):
                    at = slice(t * P, (t + 1) * P)
                    dve.wait_ge(xhi_done, t + 1)
                    dve.tensor_tensor(xt_lo[:, :, at], ps_t[:, t % 2, :, :], f32(xt_hi[:, :, at]), ALU.subtract)\
                       .then_inc(xt_split, 1)

                count = [0]

                def link(instruction):
                    count[0] += 1
                    instruction.then_inc(chain, 1)
                    dve.wait_ge(chain, count[0])

                def angles():
                    dve.wait_ge(small_loaded, 16 * (len(smalls) + 1))
                    link(dve.memset(eps_sb[:, :], EPS))
                    link(dve.tensor_copy(pos[:, :], lens_sb[:, :]))
                    link(dve.tensor_scalar(pos[:, :], pos[:, :], step_sb[:, 0:1], None, ALU.add))
                    link(dve.tensor_tensor(angle[:, :, :], pos[:, :].unsqueeze(2).to_broadcast([P, NT, H]),
                                           freq_sb[:, :].unsqueeze(1).to_broadcast([P, NT, H]), ALU.mult))

                def wrap(a, quarter):
                    r = wrapped[:, a, :, :]
                    link(dve.tensor_scalar(turns[:, :, :], angle[:, :, :], 1.0 / TWO_PI, quarter, ALU.mult, ALU.add))
                    link(dve.tensor_scalar(turns[:, :, :], turns[:, :, :], ROUND, None, ALU.add))
                    link(dve.tensor_scalar(turns[:, :, :], turns[:, :, :], -ROUND, None, ALU.add))
                    link(dve.scalar_tensor_tensor(r, turns[:, :, :], -PI_HI, angle[:, :, :], ALU.mult, ALU.add))
                    link(dve.scalar_tensor_tensor(r, turns[:, :, :], -PI_MID, r, ALU.mult, ALU.add))
                    link(dve.scalar_tensor_tensor(r, turns[:, :, :], -PI_LO, r, ALU.mult, ALU.add))
                    if a:
                        link(dve.tensor_scalar(r, r, float(np.pi / 2), None, ALU.add))
                    dve.tensor_scalar(r, r, PI_MAX, -PI_MAX, ALU.min, ALU.max).then_inc(angles_ready, 1)

                for t in range(NT):
                    x_lo(t)
                    if t == 5:
                        angles()
                    if t == 8:
                        wrap(0, 0.0)
                    if t == 12:
                        wrap(1, 0.25)

                def invert(n, j, which):
                    dve.wait_ge(rooted, n + 1)
                    dve.reciprocal(inv_rms[:, j % 2, :], rms[:, j % 2, :]).then_inc(inverted, 1)

                def add_squares(n, j, which):
                    dve.wait_ge(squared, n + 1)
                    dve.tensor_reduce(sumsq[:, j % 2, :], squares[:, j % 2, :, :], AX.X, ALU.add).then_inc(summed, 1)

                def normalise(n, j, which):
                    p = j % 2
                    dve.wait_ge(inverted, n + 1)
                    if later(n, 2):
                        dve.wait_ge(rotated_ready, n - 1)
                    dve.tensor_tensor(normed[:, p, :, :], ps_y[:, j % 4, :, :],
                                      inv_rms[:, p, :].unsqueeze(2).to_broadcast([P, 4, DH]), ALU.mult)\
                       .then_inc(normed_ready, 1)

                def same_part(n, j, which):
                    p, t = j % 2, j % NT
                    dve.wait_ge(normed_ready, n + 1)
                    dve.tensor_tensor(part_a[:, p, :, :], normed[:, p, :, :],
                                      same[:, which, t:t + 1, :].to_broadcast([P, 4, DH]), ALU.mult)\
                       .then_inc(a_ready, 1)

                def rotate(n, j):
                    p = j % 2
                    dve.wait_ge(a_ready, n + 1)
                    dve.wait_ge(b_ready, n + 1)
                    if later(n, 2):
                        dve.wait_ge(turned, n - 1)
                    dve.tensor_tensor(rotated[:, p, :, :], part_a[:, p, :, :], part_b[:, p, :, :], ALU.add)\
                       .then_inc(rotated_ready, 1)

                def pair(b):
                    if isinstance(b, int) and b == 0:
                        return
                    first = isinstance(b, int) and b == 1
                    for j in range(STEPS + (2 if is_last(b) else 0)):
                        n = STEPS * (b - 1) + j
                        before = (n - 1, (j - 1) % STEPS, int(is_last(b) and j > 0))
                        behind = not (first and j < 1) and j <= STEPS
                        if behind:
                            invert(*before)
                            normalise(*before)
                        if j < STEPS:
                            add_squares(n, j, 0)
                        if behind:
                            same_part(*before)
                        if not (first and j < 2):
                            rotate(n - 2, (j - 2) % STEPS)

                dve.wait_ge(tables, 10)
                chunk_pairs(dve, pair)

            @block.tensor
            def _(pe):
                pe.wait_ge(ident_ready, 1)

                def turn_x(t):
                    pe.wait_ge(x_loaded[t % XB], 16 * (t // XB + 1))
                    if t >= 2:
                        pe.wait_ge(xt_split, t - 1)
                    for k in range(KC):
                        last = pe.transpose(ps_t[:, t % 2, k, :], x_sb[:, t % XB, k * P:(k + 1) * P], ident[:, :])
                    last.then_inc(xt_done, 1)

                turn_x(0)
                turn_x(1)

                def multiply(j, done):
                    t, c = j % NT, j // NT
                    for k in range(KC):
                        at = slice(t * P, (t + 1) * P)
                        last = three_pass(pe, ps_y[:, j % 4, :, :].rearrange("p h d -> p (h d)"), xt_hi[:, k, at],
                                          xt_lo[:, k, at], w_hi[:, c, k, :], w_lo[:, c, k, :], k == 0, k == KC - 1)
                    last.then_inc(done, 1)

                def turn(n, j, which):
                    p = j % 2
                    pe.wait_ge(rotated_ready, n + 1)
                    if later(n, 2):
                        pe.wait_ge(out_ready, n - 1)
                    for h in range(4):
                        last = pe.transpose(ps_t[:, p, h, :], rotated[:, p, h, :], ident[:, :])
                    last.then_inc(turned, 1)

                def pair(b):
                    values = isinstance(b, int) and b == 0
                    first = isinstance(b, int) and b == 1
                    for j in range(STEPS + (3 if is_last(b) else 0)):
                        n = STEPS * (b - 1) + j
                        if j < STEPS:
                            if j % NT == 0:
                                pe.wait_ge(w_split, 2 * b + j // NT + 1)
                            if values:
                                if j + 2 < NT:
                                    turn_x(j + 2)
                                if j < NT:
                                    pe.wait_ge(xt_split, j + 1)
                                if j >= 4:
                                    pe.wait_ge(v_ready, j - 3)
                            elif first and j < 4:
                                pe.wait_ge(v_ready, STEPS - 3 + j)
                            else:
                                pe.wait_ge(normed_ready, n - 3)
                            multiply(j, v_mm_done if values else mm_done)
                        if not values and not (first and j < 3):
                            turn(n - 3, (j - 3) % STEPS, 0)

                chunk_pairs(pe, pair)


UNITS = 2 * HK
OG = 4
PPP, PIECES, PIECE_Q, PIECE_OWN, ON_POOL = 4, 6, 3, 5, 5
EARLY = 6
PIECES_AT = [(2,), (3,), (4, 5), (), (), (), (0,), (1,)]
DVE_PIECES_AT = [(), (), (), (5,), (), (), (), ()]
EARLY_PIECES = PIECES_AT[6] + PIECES_AT[7]
LATE_PIECES = sum(PIECES_AT[:EARLY], ())
PIECE_TURN = {c: n + 1 for n, c in enumerate(EARLY_PIECES + LATE_PIECES)}
CACHED = [c for c in range(PIECES) if c not in (PIECE_Q, PIECE_OWN)]
HALF = NALL // 2


def pages_of(c):
    return (NPP, 1) if c == PIECE_OWN else ((c if c < PIECE_Q else c - 1) * PPP, PPP)


def attention(nc, k_pages, v_pages, table, lens, key_at, q_t, k_own, v_own, o_t):
    with ExitStack() as ctx:
        m = Mem(nc, ctx, "att")
        ident = m.sb("ident", [P, P])
        k_raw, q_raw = m.sb("k_raw", [P, 2, NPP + 1, HK * PSIZE]), m.sb("q_raw", [P, 2, HK * P])
        k_hi, k_lo = m.sb("k_hi", [P, 2, HK, NALL], fp32r), m.sb("k_lo", [P, 2, HK, NALL], fp32r)
        q_hi, q_lo = m.sb("q_hi", [P, 2, HK, P], fp32r), m.sb("q_lo", [P, 2, HK, P], fp32r)
        v_sb, vo_sb = m.sb("v", [P, 2, NPP // 4, HK * DH]), m.sb("vo", [SEQ, 2, HK * DH])
        lens_sb, lens_f, key_sb = m.sb("lens", [P, NSEQ], i32), m.sb("lens_f", [P, NSEQ]), m.sb("key_at", [P, NKEY])
        table_sb = m.sb("table", [1, NSEQ * NPP], i32)
        mask = m.sb("mask", [P, 2, NALL])
        prob = m.sb("prob", [P, 4, NALL])
        shift, total, inv_total = m.sb("shift", [P, 4]), m.sb("total", [P, 4]), m.sb("inv_total", [P, 4])
        pt_sb, pto_sb = m.sb("pt", [P, 2, NKEY // P, P]), m.sb("pto", [SEQ, 2, P])
        o_sb = m.sb("o", [P, 2, HK, P])
        ps_s = m.ps("ps_s", [P, 2, 2, D])
        ps_pt = m.ps("ps_pt", [P, 2, NKEY // P, P])
        ps_o = m.ps("ps_o", [P, 2, OG, P])

        zeroed, ident_ready, table_loaded = m.sem("zeroed"), m.sem("ident_ready"), m.sem("table_loaded")
        small_loaded, lens_ready, mask_zeroed, mask_ready = m.sem("small_loaded"), m.sem("lens_ready"), m.sem("mask_zeroed"), m.sem("mask_ready")
        k_loaded = [m.sems(f"k_loaded{p}_", PIECES) for p in range(2)]
        v_loaded, own_v_loaded = m.sems("v_loaded", 2), m.sems("own_v_loaded", 2)
        hi_done = m.sem("hi_done")
        pool_split, dve_split = m.sem("pool_split"), m.sem("dve_split")
        s_done = m.sem("s_done")
        masked = m.sem("masked")
        exp_done, inverted, normed = m.sem("exp_done"), m.sem("inverted"), m.sem("normed")
        t_done = m.sem("t_done")
        pt_ready, pto_ready = m.sem("pt_ready"), m.sem("pto_ready")
        pv_done = m.sem("pv_done")
        o_ready, o_stored = m.sem("o_ready"), m.sems("o_stored", 2)

        def piece(c, p):
            if c == PIECE_Q:
                return q_raw[:, p, :], *(b[:, p, :, :].rearrange("p h q -> p (h q)") for b in (q_hi, q_lo))
            first, n = pages_of(c)
            return (k_raw[:, p, first:first + n, :].rearrange("p n (h k) -> p n h k", h=HK),
                    *(b[:, p, :, first * PSIZE:(first + n) * PSIZE].rearrange("p h (n k) -> p n h k", n=n)
                      for b in (k_hi, k_lo)))

        with nc.Block() as block:
            @block.sync
            def _(sp):
                sp.dma_start(lens_sb[:, :], lens).then_inc(small_loaded, 16)
                sp.dma_start(key_sb[:, :], key_at).then_inc(small_loaded, 16)

                def pages_in(s):
                    return nc.values_load_multi_w_load_instructions(
                        table_sb[:, bass.ds(s * NPP, NPP)], engines=[mybir.EngineType.SP], min_val=0,
                        max_val=NPAGE - 1, skip_runtime_bounds_check_because="block tables name pages")[1]

                def load_k(s, p):
                    pages = pages_in(s)
                    for c in PIECE_TURN:
                        if c in CACHED:
                            if later(s, 2):
                                sp.wait_ge(pool_split, ON_POOL * (s - 2) + c + 1)
                            first, n = pages_of(c)
                            for at in range(first, first + n):
                                sp.dma_start(k_raw[:, p, at, :], k_pages[bass.ds(pages[at], 1)])\
                                  .then_inc(k_loaded[p][c], 16)

                def load_v(s, p):
                    pages = pages_in(s)
                    if later(s, 2):
                        sp.wait_ge(pv_done, HK * (s - 1))
                    for n, page in enumerate(pages):
                        at = (n % 4) * PSIZE
                        sp.dma_start(v_sb[at:at + PSIZE, p, n // 4, :], v_pages[bass.ds(page, 1)])\
                          .then_inc(v_loaded[p], 16)

                sp.dma_start(table_sb[:, :], table).then_inc(table_loaded, 16)
                sp.wait_ge(table_loaded, 16)
                load_k(0, 0)
                load_v(0, 0)
                load_k(1, 1)

                def pair(i, last):
                    for p in range(2):
                        if not last:
                            load_k(2 * i + p + 2, p)
                        if not (last and p == 1):
                            load_v(2 * i + p + 1, 1 - p)

                in_pairs(sp, NSEQ // 2, pair)

            @block.gpsimd
            def _(pool):
                def load_q(s, p):
                    if later(s, 2):
                        pool.wait_ge(pool_split, ON_POOL * (s - 2) + PIECE_Q + 1)
                    pool.dma_start(q_raw[:, p, :], q_t[bass.ds(s, 1)].rearrange("s d g x -> s d (g x)"))\
                        .then_inc(k_loaded[p][PIECE_Q], 16)

                def load_own_k(s, p):
                    if later(s, 2):
                        pool.wait_ge(dve_split, s - 1)
                    pool.dma_start(k_raw[:, p, NPP, :], k_own[bass.ds(s, 1)]).then_inc(k_loaded[p][PIECE_OWN], 16)

                def load_own_v(s, p):
                    if later(s, 2):
                        pool.wait_ge(pv_done, HK * (s - 1))
                    pool.dma_start(vo_sb[:, p, :], v_own[bass.ds(s * SEQ, SEQ), :]).then_inc(own_v_loaded[p], 16)

                def store(s, p):
                    pool.wait_ge(o_ready, (HK // OG) * (s + 1))
                    pool.dma_start(o_t[bass.ds(s, 1)], o_sb[:, p, :, :].rearrange("p h q -> p (h q)"))\
                        .then_inc(o_stored[p], 16)

                for s in range(2):
                    load_q(s, s)
                    load_own_k(s, s)
                make_identity(pool, ident, zeroed, ident_ready)
                pool.memset(mask[:, :, NKEY:NALL], 0.0).then_inc(mask_zeroed, 1)

                def pair(i, last):
                    for p in range(2):
                        s = 2 * i + p
                        for c in range(ON_POOL):
                            raw, hi, lo = piece(c, p)
                            pool.wait_ge(hi_done, PIECES * s + PIECE_TURN[c])
                            pool.tensor_tensor(lo, raw, f32(hi), ALU.subtract).then_inc(pool_split, 1)
                        if not last:
                            load_q(s + 2, p)
                            load_own_k(s + 2, p)
                        load_own_v(s, p)
                        if later(s, 2):
                            store(s - 2, p)

                in_pairs(pool, NSEQ // 2, pair)
                for p in range(2):
                    store(NSEQ - 2 + p, p)
                for p in range(2):
                    pool.wait_ge(o_stored[p], 16 * NSEQ // 2)

            @block.scalar
            def _(act):
                def exponential(u, j):
                    b = j % 4
                    act.wait_ge(masked, u + 1)
                    act.activation(prob[:, b, :], prob[:, b, :], ACT.Exp, bias=shift[:, b:b + 1], scale=-1.0,
                                   accum_out=total[:, b:b + 1]).then_inc(exp_done, 1)

                def copy_pt(u, j):
                    act.wait_ge(t_done, u + 1)
                    if later(u, 2):
                        act.wait_ge(pv_done, u - 1)
                    act.activation(pt_sb[:, j % 2, :, :], ps_pt[:, j % 2, :, :], ACT.Copy).then_inc(pt_ready, 1)

                def split_hi(s, turn, p, c):
                    raw, hi, _ = piece(c, p)
                    act.wait_ge(k_loaded[p][c], 16 * (1 if c == PIECE_Q else pages_of(c)[1]) * turn)
                    if later(s, 2):
                        act.wait_ge(s_done, HK * (s - 1))
                    act.activation(hi, raw, ACT.Copy).then_inc(hi_done, 1)

                for c in PIECE_TURN:
                    split_hi(0, 1, 0, c)
                for c in EARLY_PIECES:
                    split_hi(1, 1, 1, c)
                exponential(0, 0)
                exponential(1, 1)

                def pair(i, last):
                    for j in range(UNITS):
                        u = UNITS * i + j
                        copy_pt(u, j)
                        if not (last and j >= UNITS - 2):
                            exponential(u + 2, (j + 2) % UNITS)
                        if not (last and j >= EARLY):
                            ahead = j // HK + (2 if j % HK >= EARLY else 1)
                            for c in PIECES_AT[j % HK]:
                                split_hi(2 * i + ahead, i + ahead // 2 + 1, ahead % 2, c)

                in_pairs(act, NSEQ // 2, pair)

            @block.vector
            def _(dve):
                dve.wait_ge(small_loaded, 32)
                dve.tensor_copy(lens_f[:, :], lens_sb[:, :]).then_inc(lens_ready, 1)
                dve.wait_ge(lens_ready, 1)
                dve.wait_ge(mask_zeroed, 1)

                def make_mask(s, p):
                    dve.tensor_scalar(mask[:, p, 0:NKEY], key_sb[:, :], lens_f[:, bass.ds(s, 1)], MASKED,
                                      ALU.is_ge, ALU.mult).then_inc(mask_ready, 1)
                    dve.wait_ge(mask_ready, s + 1)

                def wait_for_scores(s, u, j):
                    if j % HK == 0:
                        make_mask(s, j // HK)
                    dve.wait_ge(s_done, u + 1)
                    if later(u, 4):
                        dve.wait_ge(t_done, u - 3)

                def mask_and_max(u, j):
                    b = j % 4
                    dve.tensor_tensor_reduce(
                        out=prob[:, b, :].rearrange("p (a n) -> p a n", a=2), in0=ps_s[:, j % 2, :, 0:HALF],
                        in1=mask[:, j // HK, :].rearrange("p (a n) -> p a n", a=2), scale=-SM_SCALE, scalar=3e38, op0=ALU.add, op1=ALU.min,
                        accum_out=shift[:, b:b + 1]).then_inc(masked, 1)

                def invert(u, j):
                    dve.wait_ge(exp_done, u + 1)
                    dve.reciprocal(inv_total[:, j % 4:j % 4 + 1], total[:, j % 4:j % 4 + 1]).then_inc(inverted, 1)

                def normalise(u, j):
                    b = j % 4
                    dve.wait_ge(inverted, u + 1)
                    dve.tensor_scalar(prob[:, b, :], prob[:, b, :], inv_total[:, b:b + 1], None, ALU.mult)\
                       .then_inc(normed, 1)

                def copy_own(u, j):
                    dve.wait_ge(t_done, u + 1)
                    if later(u, 2):
                        dve.wait_ge(pv_done, u - 1)
                    dve.tensor_copy(pto_sb[:, j % 2, :], ps_s[0:SEQ, (j + 1) % 2, 1, D - P:D]).then_inc(pto_ready, 1)

                def copy_o(i, u, j):
                    p, g = j // HK, j // OG
                    dve.wait_ge(pv_done, u + 1)
                    if later(u, UNITS):
                        dve.wait_ge(o_stored[p], 16 * i)
                    dve.tensor_copy(o_sb[:, p, (g % 2) * OG:(g % 2 + 1) * OG, :], ps_o[:, g % 2, :, :])\
                       .then_inc(o_ready, 1)

                def split_lo(s, p, c):
                    raw, hi, lo = piece(c, p)
                    dve.wait_ge(hi_done, PIECES * s + PIECE_TURN[c])
                    dve.tensor_tensor(lo, raw, f32(hi), ALU.subtract).then_inc(dve_split, 1)

                for c in range(ON_POOL, PIECES):
                    split_lo(0, 0, c)
                for j in range(2):
                    wait_for_scores(0, j, j)
                    mask_and_max(j, j)
                invert(0, 0)
                normalise(0, 0)

                def pair(i, last):
                    for j in range(UNITS):
                        u = UNITS * i + j
                        if not (last and j >= UNITS - 2):
                            wait_for_scores(2 * i + (j + 2) // HK, u + 2, (j + 2) % UNITS)
                        if not (last and j >= UNITS - 1):
                            invert(u + 1, j + 1)
                        if not (last and j >= UNITS - 2):
                            mask_and_max(u + 2, (j + 2) % UNITS)
                        copy_own(u, j)
                        if not (last and j >= UNITS - 1):
                            normalise(u + 1, j + 1)
                        if not (last and j >= HK):
                            for c in DVE_PIECES_AT[j % HK]:
                                split_lo(2 * i + j // HK + 1, 1 - j // HK, c)
                        if j % OG == 1:
                            if j > 1:
                                copy_o(i, u - 2, j - 2)
                            elif later(u, UNITS):
                                copy_o(i - 1, u - 2, UNITS - 1)
                    if last:
                        copy_o(i, UNITS * i + UNITS - 1, UNITS - 1)

                in_pairs(dve, NSEQ // 2, pair)

            @block.tensor
            def _(pe):
                def scores(i, u, j):
                    p, h = j // HK, j % HK
                    if h == 0:
                        pe.wait_ge(pool_split, ON_POOL * (2 * i + p + 1))
                        pe.wait_ge(dve_split, (PIECES - ON_POOL) * (2 * i + p + 1))
                    if later(u, 2):
                        pe.wait_ge(masked, u - 1)
                    if later(u, 3):
                        pe.wait_ge(pto_ready, u - 2)
                    for half in range(2):
                        keys = slice(half * HALF, (half + 1) * HALF)
                        mm = three_pass(pe, ps_s[:, j % 2, half, 0:HALF], q_hi[:, p, h, :], q_lo[:, p, h, :],
                                        k_hi[:, p, h, keys], k_lo[:, p, h, keys], True, True)
                    mm.then_inc(s_done, 1)

                def transpose(u, j):
                    pe.wait_ge(normed, u + 1)
                    if later(u, 2):
                        pe.wait_ge(pt_ready, u - 1)
                    for c in range(NKEY // P):
                        pe.transpose(ps_pt[:, j % 2, c, :], prob[:, j % 4, c * P:(c + 1) * P], ident[:, :])
                    pe.transpose(ps_s[0:SEQ, (j + 1) % 2, 1, D - P:D], prob[:, j % 4, NKEY:NALL], ident[:, :])\
                      .then_inc(t_done, 1)

                def outputs(i, u, j):
                    p, h, g = j // HK, j % HK, j // OG
                    if h == 0:
                        pe.wait_ge(v_loaded[p], 16 * NPP * (i + 1))
                    if j % OG == 0 and later(u, 2 * OG):
                        pe.wait_ge(o_ready, (UNITS // OG) * i + g - 1)
                    pe.wait_ge(pt_ready, u + 1)
                    out = ps_o[:, g % 2, j % OG, :]
                    for c in range(NKEY // P):
                        pe.matmul(out, v_sb[:, p, c, h * DH:(h + 1) * DH], pt_sb[:, j % 2, c, :],
                                  start=(c == 0), stop=False)
                    if h == 0:
                        pe.wait_ge(own_v_loaded[p], 16 * (i + 1))
                    pe.wait_ge(pto_ready, u + 1)
                    pe.matmul(out, vo_sb[:, p, h * DH:(h + 1) * DH], pto_sb[:, j % 2, :],
                              start=False, stop=True).then_inc(pv_done, 1)

                pe.wait_ge(ident_ready, 1)
                scores(0, 0, 0)
                scores(0, 1, 1)

                def pair(i, last):
                    for j in range(UNITS):
                        u = UNITS * i + j
                        if not (last and j >= UNITS - 2):
                            scores(i + (j + 2) // UNITS, u + 2, (j + 2) % UNITS)
                        transpose(u, j)
                        if j > 0:
                            outputs(i, u - 1, j - 1)
                        elif later(u, 1):
                            outputs(i - 1, u - 1, UNITS - 1)
                    if last:
                        outputs(i, UNITS * i + UNITS - 1, UNITS - 1)

                in_pairs(pe, NSEQ // 2, pair)


def output_projection(nc, x_in, o_t, w, x_out):
    HH = HQ // 2
    WG = 4
    GROUPS, STAGES = HQ // WG, 4
    with ExitStack() as ctx:
        m = Mem(nc, ctx, "out")
        w_stage = m.sb("w_stage", [P, STAGES, WG, D])
        w_hi, w_lo = m.sb("w_hi", [P, HQ, D], fp32r), m.sb("w_lo", [P, HQ, D], fp32r)
        o_sb = m.sb("o", [P, SPT, HH, SEQ])
        oh_sb, ol_sb = m.sb("o_hi", [P, 2, HH, P], fp32r), m.sb("o_lo", [P, 2, HH, P], fp32r)
        x_sb, y_sb = m.sb("x", [P, D]), m.sb("y", [P, D])
        ps_y = m.ps("ps_y", [P, 2, D])

        w_loaded = m.sems("w_loaded", STAGES)
        w_hi_done, w_split = m.sem("w_hi_done"), m.sem("w_split")
        o_loaded, x_loaded = m.sem("o_loaded"), m.sem("x_loaded")
        hi_done, split_done = m.sem("hi_done"), m.sem("split_done")
        half_done = m.sem("half_done")
        y_ready, y_stored = m.sem("y_ready"), m.sem("y_stored")

        with nc.Block() as block:
            @block.sync
            def _(sp):
                def load_o(t, half):
                    sp.dma_start(o_sb[:, :, :, :].rearrange("p s h q -> p s (h q)"),
                                 o_t[bass.ds(t * SPT, SPT), :, half * HH * SEQ:(half + 1) * HH * SEQ]
                                 .rearrange("s d n -> d s n")).then_inc(o_loaded, 16)

                def load_w(g):
                    if g >= STAGES:
                        sp.wait_ge(w_split, g - STAGES + 1)
                    sp.dma_start(w_stage[:, g % STAGES, :, :], w[g]).then_inc(w_loaded[g % STAGES], 16)

                load_o(0, 0)
                for g in range(GROUPS // 2):
                    load_w(g)
                sp.wait_ge(split_done, 1)
                load_o(0, 1)
                for g in range(GROUPS // 2, GROUPS):
                    load_w(g)
                sp.dma_start(x_sb[:, :], x_in[0:P, :]).then_inc(x_loaded, 16)

                def pair(i, last):
                    for p in range(2):
                        t = 2 * i + p
                        if later(t, 1):
                            sp.wait_ge(split_done, 2 * t + 1)
                            load_o(t, 1)
                        sp.wait_ge(split_done, 2 * t + 2)
                        if not (last and p):
                            load_o(t + 1, 0)
                        sp.wait_ge(y_ready, t + 1)
                        sp.dma_start(x_out[bass.ds(t * P, P), :], y_sb[:, :]).then_inc(y_stored, 16)
                        if not (last and p):
                            sp.dma_start(x_sb[:, :], x_in[bass.ds((t + 1) * P, P), :]).then_inc(x_loaded, 16)

                in_pairs(sp, NT // 2, pair)
                sp.wait_ge(y_stored, 16 * NT)

            @block.scalar
            def _(act):
                def split_w_hi(g):
                    act.wait_ge(w_loaded[g % STAGES], 16 * (g // STAGES + 1))
                    act.activation(w_hi[:, g * WG:(g + 1) * WG, :], w_stage[:, g % STAGES, :, :], ACT.Copy)\
                       .then_inc(w_hi_done, 1)

                def split_hi(n, p):
                    act.wait_ge(o_loaded, 16 * (n + 1))
                    if later(n, 2):
                        act.wait_ge(half_done, n - 1)
                    act.activation(oh_sb[:, p, :, :].rearrange("p h (s q) -> p s h q", s=SPT),
                                   o_sb[:, :, :, :], ACT.Copy).then_inc(hi_done, 1)

                for g in range(GROUPS):
                    if g % (GROUPS // 2) == 0:
                        split_hi(g // (GROUPS // 2), g // (GROUPS // 2))
                    split_w_hi(g)

                def pair(i, last):
                    for j in range(4):
                        if later(i, 1) or j >= 2:
                            split_hi(4 * i + j, j % 2)

                in_pairs(act, NT // 2, pair)

            @block.vector
            def _(dve):
                def split_w_lo(g):
                    at = slice(g * WG, (g + 1) * WG)
                    dve.wait_ge(w_hi_done, g + 1)
                    dve.tensor_tensor(w_lo[:, at, :], w_stage[:, g % STAGES, :, :], f32(w_hi[:, at, :]), ALU.subtract)\
                       .then_inc(w_split, 1)

                def split_lo(n, p):
                    dve.wait_ge(hi_done, n + 1)
                    dve.tensor_tensor(ol_sb[:, p, :, :].rearrange("p h (s q) -> p s h q", s=SPT), o_sb[:, :, :, :],
                                      f32(oh_sb[:, p, :, :]).rearrange("p h (s q) -> p s h q", s=SPT),
                                      ALU.subtract).then_inc(split_done, 1)

                def add(t, p):
                    dve.wait_ge(half_done, 2 * t + 2)
                    dve.wait_ge(x_loaded, 16 * (t + 1))
                    if later(t, 1):
                        dve.wait_ge(y_stored, 16 * t)
                    dve.tensor_tensor(y_sb[:, :], ps_y[:, p, :], x_sb[:, :], ALU.add).then_inc(y_ready, 1)

                for g in range(GROUPS):
                    if g % (GROUPS // 2) == 0:
                        split_lo(g // (GROUPS // 2), g // (GROUPS // 2))
                    split_w_lo(g)

                def pair(i, last):
                    for p in range(2):
                        t = 2 * i + p
                        if not (last and p):
                            split_lo(2 * t + 2, 0)
                        add(t, p)
                        if not (last and p):
                            split_lo(2 * t + 3, 1)

                in_pairs(dve, NT // 2, pair)

            @block.tensor
            def _(pe):
                def pair(i, last):
                    for p in range(2):
                        t = 2 * i + p
                        if later(t, 2):
                            pe.wait_ge(y_ready, t - 1)
                        for half in range(2):
                            pe.wait_ge(split_done, 2 * t + half + 1)
                            for h in range(HH):
                                if not later(t, 1) and h % WG == 0:
                                    pe.wait_ge(w_split, (half * HH + h) // WG + 1)
                                mm = three_pass(pe, ps_y[:, p, :], oh_sb[:, half, h, :], ol_sb[:, half, h, :],
                                                w_hi[:, half * HH + h, :], w_lo[:, half * HH + h, :],
                                                half == 0 and h == 0, half == 1 and h == HH - 1)
                            mm.then_inc(half_done, 1)

                in_pairs(pe, NT // 2, pair)


def conditioned_stack(nc, i, out):
    def scratch(name, shape):
        return nc.dram_tensor(name, shape, fp32, kind="Internal").ap()

    x1, x2, x3 = scratch("x1", [TOK, D]), scratch("x2", [TOK, D]), scratch("x3", [TOK, D])
    q_t, k_own = scratch("q_t", [NSEQ, DH, HK, REP * SEQ]), scratch("k_own", [NSEQ, DH, 2, 4 * SEQ])
    v_own, o_t = scratch("v_own", [TOK, HK * DH]), scratch("o_t", [NSEQ, DH, HQ * SEQ])
    layer0(nc, i["x"], i["ids0"], i["w0"], x1)
    lora_layer(nc, "l1", 1, x1, i["w1"], i["bias1"], i["a1"], i["b1"], i["ids1"], i["slots1"], i["factor1"], x2)
    lora_layer(nc, "l2", NAD2 * RANK // P, x2, i["w2"], i["bias2"], i["a2"], i["b2"], i["ids2"], i["slots2"],
               i["factor2"], x3)
    qkv(nc, x3, i["w_qkv"], i["lens_tok"], i["inv_freq"], i["step_pos"], i["norm_w"], q_t, k_own, v_own)
    attention(nc, i["k_pages"], i["v_pages"], i["table"], i["lens_all"], i["key_at"], q_t,
              k_own.rearrange("s d c x -> s d (c x)"), v_own, o_t)
    output_projection(nc, x3, o_t, i["wo"], out)


def laid_out(a):
    def chunked(w_t):
        return w_t.reshape(KC, P, -1).transpose(1, 0, 2)

    def everywhere(v):
        return np.broadcast_to(v.reshape(1, -1), (P, v.size))

    lens = a["itok_B_207_1644"]
    w_qkv = np.concatenate([a["L3_cond_Wv"], a["L3_cond_Wq"], a["L3_cond_Wk"]], axis=0)
    return {
        "x": a["x"].reshape(TOK, D),
        "ids0": a["itok_B_3_7"].reshape(1, NSEQ),
        "w0": a["L0_cond_weight"].transpose(0, 2, 1).reshape(NAD0, KC, P, D).transpose(0, 2, 1, 3),
        "w1": chunked(a["L1_cond_weight"].T),
        "bias1": everywhere(a["L1_cond_bias"]),
        "a1": chunked(a["L1_cond_lora_a_weights"].reshape(NAD1 * RANK, D).T),
        "b1": a["L1_cond_lora_b_weights"].transpose(0, 2, 1).reshape(1, P, D).transpose(1, 0, 2),
        "ids1": everywhere(a["itok_B_1_7"]),
        "slots1": (np.arange(P) // RANK).reshape(P, 1).astype(np.float32),
        "factor1": np.repeat(a["L1_cond_scaling_factors"], RANK).reshape(P, 1),
        "w2": chunked(a["L2_cond_W"].T),
        "bias2": everywhere(a["L2_cond_b"]),
        "a2": chunked(a["L2_cond_lora_As"].transpose(1, 0, 2).reshape(D, NAD2 * RANK)),
        "b2": a["L2_cond_lora_Bs"].reshape(NAD2 * RANK // P, P, D).transpose(1, 0, 2),
        "ids2": everywhere(a["itok_B_0_23"]),
        "slots2": (np.arange(NAD2 * RANK) // RANK).reshape(-1, P).T.astype(np.float32),
        "factor2": np.full((P, 1), 32 / RANK, np.float32),
        "w_qkv": w_qkv.reshape(W3, D, KC, P).transpose(0, 3, 2, 1),
        "lens_tok": np.repeat(lens.reshape(NT, SPT), SEQ, axis=1).T,
        "inv_freq": everywhere((1.0 / 10000.0 ** (np.arange(0, DH, 2) / DH)).astype(np.float32)),
        "step_pos": (np.arange(P) % SEQ).astype(np.float32).reshape(P, 1),
        "norm_w": np.broadcast_to(np.stack([a["L3_cond_q_norm_w"], a["L3_cond_k_norm_w"]]), (P, 2, DH)),
        "k_pages": a["L3_cond_k_cache"].transpose(0, 3, 2, 1).reshape(NPAGE, DH, HK * PSIZE),
        "v_pages": a["L3_cond_v_cache"].reshape(NPAGE, PSIZE, HK * DH),
        "table": a["itok_Bx16_0_63"].reshape(1, -1),
        "lens_all": everywhere(lens),
        "key_at": everywhere(np.arange(NKEY).astype(np.float32)),
        "wo": a["L3_cond_Wo"].T.reshape(8, HQ // 8, DH, D).transpose(0, 2, 1, 3),
    }


def kernel(**inputs):
    import concourse.bacc as bacc
    from concourse.bass_utils import run_bass_kernel_spmd

    arrays = {f"in_{name}": np.ascontiguousarray(v)
              for name, v in laid_out({k: np.asarray(v) for k, v in inputs.items()}).items()}
    nc = bacc.Bacc("TRN2", target_bir_lowering=False, num_devices=1)
    aps = {name[3:]: nc.dram_tensor(name, v.shape, mybir.dt.from_np(v.dtype), kind="ExternalInput").ap()
           for name, v in arrays.items()}
    out = nc.dram_tensor("out", (TOK, D), fp32, kind="ExternalOutput").ap()
    conditioned_stack(nc, aps, out)
    r = run_bass_kernel_spmd(nc, [arrays], core_ids=[0])
    return r.results[0]["out"].reshape(NSEQ, SEQ, D)
```
